# Optimizing a Trainium2 kernel written in Bass

```python
import numpy as np
import jax
import jax.numpy as jnp

def _softmax(x, axis=-1):
    return jax.nn.softmax(x, axis=axis)

def _gelu(x):
    return jax.nn.gelu(x, approximate=True)

def _silu(x):
    return jax.nn.silu(x)

def _sigmoid(x):
    return jax.nn.sigmoid(x)

def _layernorm(x, axis=-1, eps=1e-05):
    m = jnp.mean(x, axis=axis, keepdims=True)
    v = jnp.var(x, axis=axis, keepdims=True)
    return (x - m) / jnp.sqrt(v + eps)

def _scatter_add(tgt, idx, src, axis=0):
    return tgt.at[idx].add(src)

def _segment_sum(src, seg, n):
    return jax.ops.segment_sum(src, seg, n)
kernel_name = 'mk_gnn_resnorm_d1_gnn_r8_9e3543'

def setup_inputs(seed: int=0):
    np.random.seed(seed)
    _w = jnp.asarray

    def _rec_inputs():
        import jax
        import jax.numpy as jnp
        _gk = jax.random.key(seed)
        x = -0.0005963 + 1.001 * jax.random.normal(jax.random.fold_in(_gk, 1), (384, 1024), jnp.float32)
        src = jax.random.randint(jax.random.fold_in(_gk, 2), (6144,), 0, 384, jnp.int32)
        dst = jax.random.randint(jax.random.fold_in(_gk, 3), (6144,), 0, 384, jnp.int32)
        _o = jnp.argsort(dst, stable=True)
        src = src[_o]
        dst = dst[_o]
        edge_type_5 = jax.random.randint(jax.random.fold_in(_gk, 12), (6144,), 0, 5, jnp.int32)
        return (x, src, dst, edge_type_5)
    x, src, dst, edge_type_5 = _rec_inputs()

    def _L0_gnn_setup():
        import jax, jax.numpy as jnp
        import numpy as np
        N = 384
        E = 12288
        IN_F = 1024
        OUT_F = 1024
        H = 16
        D = OUT_F // H
        NUM_ETYPES = 4

        def _build_mask(edge_index, edge_type, edge_type_weights, dtype):
            src, dst = (edge_index[0], edge_index[1])
            w = jax.nn.softplus(edge_type_weights)
            mask = jnp.full((N, N), -jnp.inf, dtype=dtype)
            mask = mask.at[src, dst].set(w[edge_type - 1])
            diag = jnp.diagonal(mask)
            idx = jnp.arange(N)
            mask = mask.at[idx, idx].set(jnp.where(jnp.isneginf(diag), w[3], diag))
            return mask
        key = jax.random.key(seed)
        ks = jax.random.split(key, 20)
        p = lambda k, shape: jax.random.normal(k, shape, dtype=jnp.float32) * 0.02
        return {'x': jax.random.normal(ks[0], (N, IN_F), dtype=jnp.float32), 'edge_index': jax.random.randint(ks[1], (2, E), 0, N), 'edge_type': jax.random.randint(ks[2], (E,), 1, NUM_ETYPES + 1), 'edge_type_weights': jnp.ones((NUM_ETYPES,), jnp.float32) + 0.1 * jax.random.normal(ks[3], (NUM_ETYPES,), dtype=jnp.float32), 'wq': p(ks[4], (OUT_F, IN_F)), 'bq': p(ks[5], (OUT_F,)), 'wk': p(ks[6], (OUT_F, IN_F)), 'bk': p(ks[7], (OUT_F,)), 'wv': p(ks[8], (OUT_F, IN_F)), 'bv': p(ks[9], (OUT_F,)), 'wiq': p(ks[10], (OUT_F, OUT_F)), 'biq': p(ks[11], (OUT_F,)), 'wik': p(ks[12], (OUT_F, OUT_F)), 'bik': p(ks[13], (OUT_F,)), 'wiv': p(ks[14], (OUT_F, OUT_F)), 'biv': p(ks[15], (OUT_F,)), 'wo': p(ks[16], (OUT_F, OUT_F)), 'bo': p(ks[17], (OUT_F,))}
    _L0_gnn_all = _L0_gnn_setup()
    _L0_gnn_in = {k: v for k, v in _L0_gnn_all.items() if k in ('edge_type_weights', 'wq', 'bq', 'wk', 'bk', 'wv', 'bv', 'wiq', 'biq', 'wik', 'bik', 'wiv', 'biv', 'wo', 'bo')}
    del _L0_gnn_all
    return {'x': x, 'src': src, 'dst': dst, 'edge_type_5': edge_type_5, 'L0_gnn_edge_type_weights': _L0_gnn_in['edge_type_weights'], 'L0_gnn_wq': _L0_gnn_in['wq'], 'L0_gnn_bq': _L0_gnn_in['bq'], 'L0_gnn_wk': _L0_gnn_in['wk'], 'L0_gnn_bk': _L0_gnn_in['bk'], 'L0_gnn_wv': _L0_gnn_in['wv'], 'L0_gnn_bv': _L0_gnn_in['bv'], 'L0_gnn_wiq': _L0_gnn_in['wiq'], 'L0_gnn_biq': _L0_gnn_in['biq'], 'L0_gnn_wik': _L0_gnn_in['wik'], 'L0_gnn_bik': _L0_gnn_in['bik'], 'L0_gnn_wiv': _L0_gnn_in['wiv'], 'L0_gnn_biv': _L0_gnn_in['biv'], 'L0_gnn_wo': _L0_gnn_in['wo'], 'L0_gnn_bo': _L0_gnn_in['bo']}

def reference(x, src, dst, edge_type_5, L0_gnn_edge_type_weights, L0_gnn_wq, L0_gnn_bq, L0_gnn_wk, L0_gnn_bk, L0_gnn_wv, L0_gnn_bv, L0_gnn_wiq, L0_gnn_biq, L0_gnn_wik, L0_gnn_bik, L0_gnn_wiv, L0_gnn_biv, L0_gnn_wo, L0_gnn_bo):
    import jax
    import jax.numpy as jnp

    def _L0_gnn_ref(x, edge_index, edge_type, edge_type_weights, wq, bq, wk, bk, wv, bv, wiq, biq, wik, bik, wiv, biv, wo, bo):
        import jax, jax.numpy as jnp
        import numpy as np
        N = 384
        E = 12288
        IN_F = 1024
        OUT_F = 1024
        H = 16
        D = OUT_F // H
        NUM_ETYPES = 4

        def _build_mask(edge_index, edge_type, edge_type_weights, dtype):
            src, dst = (edge_index[0], edge_index[1])
            w = jax.nn.softplus(edge_type_weights)
            mask = jnp.full((N, N), -jnp.inf, dtype=dtype)
            mask = mask.at[src, dst].set(w[edge_type - 1])
            diag = jnp.diagonal(mask)
            idx = jnp.arange(N)
            mask = mask.at[idx, idx].set(jnp.where(jnp.isneginf(diag), w[3], diag))
            return mask
        q = x @ wq.T + bq
        k = x @ wk.T + bk
        v = x @ wv.T + bv
        q2 = (q @ wiq.T + biq).reshape(N, H, D).transpose(1, 0, 2)
        k2 = (k @ wik.T + bik).reshape(N, H, D).transpose(1, 0, 2)
        v2 = (v @ wiv.T + biv).reshape(N, H, D).transpose(1, 0, 2)
        mask = _build_mask(edge_index, edge_type, edge_type_weights, x.dtype)
        scale = 1.0 / np.sqrt(D).astype(np.float32)
        scores = jnp.einsum('hnd,hmd->hnm', q2, k2) * scale + mask[None]
        attn = jax.nn.softmax(scores, axis=-1)
        out = jnp.einsum('hnm,hmd->hnd', attn, v2)
        out = out.transpose(1, 0, 2).reshape(N, OUT_F)
        return out @ wo.T + bo
    edge_index = jnp.stack([src, dst])
    x = _layernorm(x + _L0_gnn_ref(x, edge_index, edge_type_5, L0_gnn_edge_type_weights, L0_gnn_wq, L0_gnn_bq, L0_gnn_wk, L0_gnn_bk, L0_gnn_wv, L0_gnn_bv, L0_gnn_wiq, L0_gnn_biq, L0_gnn_wik, L0_gnn_bik, L0_gnn_wiv, L0_gnn_biv, L0_gnn_wo, L0_gnn_bo), axis=-1)
    return x

_drawn_inputs = setup_inputs


def setup_inputs(seed=0):
    import zlib

    import numpy as np

    out = dict(_drawn_inputs(seed))
    spreads = {}
    factors = {'L0_gnn_edge_type_weights': 28.539,
     'L0_gnn_wq': 5.221,
     'L0_gnn_bq': 8.0,
     'L0_gnn_wk': 5.217,
     'L0_gnn_bk': 64.0,
     'L0_gnn_bv': 7.157,
     'L0_gnn_wiq': 5.218,
     'L0_gnn_biq': 8.0,
     'L0_gnn_wik': 5.209,
     'L0_gnn_bik': 64.0,
     'L0_gnn_biv': 4.508,
     'L0_gnn_bo': 2.875}
    for name, (base, spread) in spreads.items():
        noise = np.random.default_rng([zlib.crc32(name.encode()), seed]).standard_normal(out[name].shape)
        drawn = base * np.exp(spread * noise) if base else spread * noise
        out[name] = jnp.asarray(drawn.astype(out[name].dtype))
    for name, factor in factors.items():
        out[name] = (out[name] * factor).astype(out[name].dtype)
    return out
```

```python
from contextlib import ExitStack

import concourse.bass as bass
import numpy as np
from concourse import mybir

F32 = mybir.dt.float32
F32R = mybir.dt.float32r
BF16 = mybir.dt.bfloat16
FP16 = mybir.dt.float16
I32 = mybir.dt.int32
ACT = mybir.ActivationFunctionType
ALU = mybir.AluOpType
AX_X = mybir.AxisListType.X
ds = bass.ds

P = 128
N = 384
NT = N // P
F = 1024
KT = F // P
HEADS = 16
D = F // HEADS
PAIRS = HEADS // 2
HALF = 512
ETYPES = 4
LN_EPS = 1e-5

E = 6144
CHUNKS = E // P
GC = 8
GROUPS = CHUNKS // GC
GE = GC * P
PACK = 8
DH = N // PACK

RING = 4
L1_TILES = 3 * KT
IV_TILE = L1_TILES
PAIR_TILE = IV_TILE + KT
WO_TILE = PAIR_TILE + 2 * PAIRS
TILES = WO_TILE + KT
LEAD = 2
POOL_COLS = 448
NEG = -3.0e38
SCALE = 1.0 / 8.0

BITS = slice(0, DH)
CODES = slice(DH, 2 * DH)


def gnn_layer(nc, x_t, x_rows, weights, bias_cols, bias_rows, edge_weights, edge_cols, edge_rows,
              key_rows, src_rows, out):
    with ExitStack() as ctx:
        def sb(name, shape, dt):
            return ctx.enter_context(nc.sbuf_tensor(name, shape, dt))

        def sem(name):
            return ctx.enter_context(nc.semaphore(name))

        x_hi, x_lo = sb("x_hi", [P, KT, N], F32R), sb("x_lo", [P, KT, N], F32R)
        att_hi, att_lo = x_hi, x_lo
        h_hi, h_lo = sb("h_hi", [P, L1_TILES, N], F32R), sb("h_lo", [P, L1_TILES, N], F32R)
        V0 = 2 * KT
        qk_hi, qk_lo = h_hi[:, V0:V0 + 4, :], h_lo[:, V0:V0 + 4, :]
        pt_hi, pt_lo = h_hi[:, V0 + 4:V0 + 7, :], h_lo[:, V0 + 4:V0 + 7, :]
        w_raw = sb("w_raw", [P, RING, F], F32)
        w_hi, w_lo = sb("w_hi", [P, RING, F], F32R), sb("w_lo", [P, RING, F], F32R)
        v2 = sb("v2", [P, NT, F], F32)
        vp_hi, vp_lo = sb("vp_hi", [P, 2, NT, 3 * D], F32R), sb("vp_lo", [P, 2, NT, 3 * D], F32R)
        probs = sb("probs", [P, 2 * NT, N], F32)
        mask = sb("mask", [P, NT, N], F32)
        ident = sb("ident", [P, P], F32)
        res = sb("res", [P, NT, F], F32)
        row = sb("row", [P, F], F32)
        bcol = sb("bcol", [P, L1_TILES + 2 * PAIRS], F32)
        neg_max, row_sum, row_inv = (sb(n, [P, 2 * NT], F32) for n in ("neg_max", "row_sum", "row_inv"))
        stats = sb("stats", [P, NT, 12], F32)
        mean_var = sb("mean_var", [P, NT, 2], F32)
        std = sb("std", [P, NT], F32)
        rstd = sb("rstd", [P, NT], F32)
        v2_flat = v2[:, :, :].rearrange("p a b -> p (a b)")

        def x_raw(s):
            return v2_flat[:, 2 * N * s:2 * N * (s + 1)].rearrange("p (k n) -> p k n", k=2)

        v2_16 = v2_flat.bitcast(BF16)
        node_hot = v2_16[:, 0:NT * GE].rearrange("p (t e) -> p t e", t=NT)
        edge_hot = v2_16[:, NT * GE:2 * NT * GE].rearrange("p (c s) -> p c s", c=GC)
        keyb = probs[:, :, :].rearrange("p a b -> p (a b)")[:, 0:2 * GE].rearrange("p (s e) -> p s e", s=2)
        res_flat = res[:, :, :].rearrange("p a b -> p (a b)")
        srcb = res_flat[:, 0:GE].bitcast(FP16).rearrange("p (s e) -> p s e", s=2)
        later = res_flat[:, GE:GE + GE // 2].bitcast(BF16)
        sel, picked = (res_flat[:, GE + GE // 2 + i * N:GE + GE // 2 + (i + 1) * N].rearrange("p (c d) -> p c d", c=GC)
                       for i in range(2))
        ec = sb("ec", [P, 3, CHUNKS], I32)
        er = sb("er", [CHUNKS, 2, P], I32)
        er_key = sb("er_key", [CHUNKS, P], F32)
        er_src = sb("er_src", [CHUNKS, P], FP16)
        srcf, dstf, key = (sb(n, [P, CHUNKS], F32) for n in ("srcf", "dstf", "key"))
        dhi, dlo3, bit, one_i, code_i, packed_i = (
            sb(n, [P, CHUNKS], I32) for n in ("dhi", "dlo3", "bit", "one_i", "code_i", "packed_i"))
        dlo = sb("dlo", [P, CHUNKS], I32)
        four = sb("four", [P, CHUNKS], F32)
        bitf, codef = sb("bitf", [P, CHUNKS], F32), sb("codef", [P, CHUNKS], F32)
        iota_i = sb("iota_i", [P, N], I32)
        iota_h = sb("iota_h", [P, N], FP16)
        unread = res_flat[:, 3 * GE - 3 * GE // 4:3 * GE].bitcast(mybir.dt.uint8).rearrange("p (s e) -> p s e", s=3)
        node_i = sb("node_i", [P, NT], I32)
        node_f = sb("node_f", [P, NT], F32)
        mov = sb("mov", [P, GC, 2 * DH], BF16)
        table = sb("table", [P, NT, 2 * DH], F32)
        table_bits = sb("table_bits", [P, NT, DH], BF16)
        n_later = sb("n_later", [P, GC], F32)
        occ, occ_i, hit = sb("occ", [P, GC], F32), sb("occ_i", [P, GC], I32), sb("hit", [P, GC], I32)
        lose, win_bit, win_code = (sb(n, [P, GC], F32) for n in ("lose", "win_bit", "win_code"))
        ew, ew_abs, ew_exp, ew_ln, ew_pos, soft = (
            sb(n, [P, ETYPES], F32) for n in ("ew", "ew_abs", "ew_exp", "ew_ln", "ew_pos", "soft"))
        tab_i = sb("tab_i", [P, NT, DH], I32)
        ident4 = sb("ident4", [P, P], F32)
        diag = picked.rearrange("p c d -> p (c d)").rearrange("p (t n) -> p t n", t=NT)
        field = probs[:, 0:NT, :].bitcast(I32).rearrange("p t (d r) -> p t d r", r=PACK)
        pick1 = probs[:, 0:NT, :]
        codes = probs[:, NT:2 * NT, :]

        bank = [ctx.enter_context(nc.psum_tensor(f"bank{i}", [P, HALF], F32)) for i in range(8)]
        acc = bank[6:8]
        gather_ps = bank[0][:, 0:GC * DH].rearrange("p (c d) -> p c d", c=GC)
        scatter_ps = bank[1][:, 0:NT * 2 * DH].rearrange("p (t d) -> p t d", t=NT)

        def v_pair(a):
            return v2[:, :, ds(a * P, P)].rearrange("p n (h d) -> p n h d", h=2)

        def v_split(vp, par):
            return vp[:, par, :, :].rearrange("p n (z d) -> p n z d", z=3)[:, :, 0:3:2, :]

        def y_bank(n, h):
            return bank[6 + h] if n == 0 else bank[2 * (n - 1) + h]

        raw_loaded = [sem(f"raw_loaded{s}") for s in range(RING)]
        x_loaded = [sem(f"x_loaded{s}") for s in range(4)]
        small_loaded = sem("small_loaded")
        edges_loaded = sem("edges_loaded")
        scratch_stored = sem("scratch_stored")
        rows_loaded = sem("rows_loaded")
        res_loaded = sem("res_loaded")
        bo_loaded = sem("bo_loaded")
        x_hi_done, x_lo_done = sem("x_hi_done"), sem("x_lo_done")
        w_hi_done, w_lo_dve, w_lo_pool = sem("w_hi_done"), sem("w_lo_dve"), sem("w_lo_pool")
        tile_done = sem("tile_done")
        acc_hi = sem("acc_hi")
        acc_free = sem("acc_free")
        consts = sem("consts")
        edge_prep = sem("edge_prep")
        at_ready, a_ready, mov_ready, table_ready = (
            sem(n) for n in ("at_ready", "a_ready", "mov_ready", "table_ready"))
        gathered, scattered = sem("gathered"), sem("scattered")
        soft_a, soft_b, soft_pos = sem("soft_a"), sem("soft_b"), sem("soft_pos")
        mask_built = sem("mask_built")
        v2_acc, v2_ready = sem("v2_acc"), sem("v2_ready")
        vp_hi_done, vp_lo_done = sem("vp_hi_done"), sem("vp_lo_done")
        scores_seen = sem("scores_seen")
        scores_ready, masked, exp_done, probs_ready = (
            sem(n) for n in ("scores_ready", "masked", "exp_done", "probs_ready"))
        pt_ready, pt_hi_done, pt_lo_done, pv_done = (
            sem(n) for n in ("pt_ready", "pt_hi_done", "pt_lo_done", "pv_done"))
        att_hi_done, att_lo_done = sem("att_hi_done"), sem("att_lo_done")
        res_ready = sem("res_ready")
        y_ready, var_ready, std_ready, out_ready = (
            sem(n) for n in ("y_ready", "var_ready", "std_ready", "out_ready"))
        stored = sem("stored")
        dve_step = sem("dve_step")
        act_step = sem("act_step")
        pool_step = sem("pool_step")

        block = ctx.enter_context(nc.Block())

        @block.sync
        def _(sp):
            for s in range(4):
                sp.dma_start(x_raw(s), x_t[:, 2 * s:2 * s + 2, :]).then_inc(x_loaded[s], 16)
                sp.dma_start(w_raw[:, s, :], weights[s, :, :]).then_inc(raw_loaded[s], 16)

            def load_tile(t, s):
                sp.wait_ge(w_hi_done, t - RING + 1)
                sp.wait_ge(w_lo_dve, t - RING + 1)
                sp.wait_ge(w_lo_pool, t - RING + 1)
                sp.dma_start(w_raw[:, s, :], weights[ds(t, 1), :, :].rearrange("a p n -> (a p) n"))\
                  .then_inc(raw_loaded[s], 16)

            def load_rows(g, slot):
                sp.dma_start(keyb[:, slot, :], key_rows[ds(g, 1), :].to_broadcast([P, GE]))\
                  .then_inc(rows_loaded, 16)
                sp.dma_start(srcb[:, slot, :], src_rows[ds(g, 1), :].to_broadcast([P, GE]))\
                  .then_inc(rows_loaded, 16)

            sp.wait_ge(edge_prep, 1)
            sp.dma_start(key_rows.rearrange("g (c e) -> (g c) e", e=P), er_key[:, :]).then_inc(scratch_stored, 16)
            sp.dma_start(src_rows.rearrange("g (c e) -> (g c) e", e=P), er_src[:, :]).then_inc(scratch_stored, 16)
            sp.wait_ge(scratch_stored, 32)
            load_rows(0, 0)
            with sp.Fori(1, GROUPS) as g:
                sp.wait_ge(rows_loaded, 32 * g)
                sp.wait_ge(a_ready, g)
                load_rows(g, ds(g % 2, 1))
                for s in range(RING):
                    load_tile(4 * g + s, s)
            with sp.Fori(GROUPS, TILES // RING) as g:
                for s in range(RING):
                    load_tile(4 * g + s, s)
            for n in range(NT):
                sp.wait_ge(out_ready, n + 1)
                sp.dma_start(out[n * P:(n + 1) * P, :], res[:, n, :]).then_inc(stored, 16)
            sp.wait_ge(stored, 16 * NT)

        @block.gpsimd
        def _(pool):
            nc.gpsimd.iota(iota_i[:, :], pattern=[[1, N]], base=0, channel_multiplier=0).then_inc(consts, 1)
            nc.gpsimd.iota(node_i[:, :], pattern=[[P, NT]], base=0, channel_multiplier=1).then_inc(consts, 1)
            nc.gpsimd.memset(later[:, :], 1.0).then_inc(pool_step, 1)
            nc.gpsimd.memset(ident[:, :], 0.0).then_inc(pool_step, 1)
            pool.wait_ge(pool_step, 2)
            nc.gpsimd.affine_select(out=later[:, :], in_=later[:, :], compare_op=ALU.is_gt, fill=0.0, base=0,
                                    pattern=[[1, GE]], channel_multiplier=-1).then_inc(consts, 1)
            nc.gpsimd.affine_select(out=ident[:, :], in_=ident[:, :], compare_op=ALU.not_equal, fill=1.0, base=0,
                                    pattern=[[1, P]], channel_multiplier=-1).then_inc(consts, 1)

            def low_part(t, s):
                pool.wait_ge(w_hi_done, t + 1)
                nc.gpsimd.tensor_tensor(w_lo[:, s, 0:POOL_COLS], w_raw[:, s, 0:POOL_COLS],
                                        w_hi[:, s, 0:POOL_COLS].bitcast(F32), ALU.subtract)\
                    .then_inc(w_lo_pool, 1)

            with pool.Fori(0, 10) as g:
                for s in range(RING):
                    low_part(RING * g + s, s)
            pool.wait_ge(res_loaded, 16)
            pool.wait_ge(bo_loaded, 16)
            for n in range(NT):
                nc.gpsimd.tensor_tensor(res[:, n, :], res[:, n, :], row[:, :], ALU.add).then_inc(res_ready, 1)
            with pool.Fori(10, TILES // RING) as g:
                for s in range(RING):
                    low_part(RING * g + s, s)

        @block.scalar
        def _(act):
            act.dma_start(er[:, :, :], edge_rows).then_inc(edges_loaded, 16)
            act.dma_start(ec[:, :, :], edge_cols).then_inc(edges_loaded, 16)
            act.dma_start(ew[:, :], edge_weights.to_broadcast([P, ETYPES])).then_inc(small_loaded, 16)
            act.dma_start(bcol[:, :], bias_cols).then_inc(small_loaded, 16)
            act.dma_start(row[:, :], bias_rows[0:1, :].to_broadcast([P, F])).then_inc(small_loaded, 16)

            def high_part(t, s, raws):
                act.wait_ge(raw_loaded[s], 16 * raws)
                nc.scalar.activation(w_hi[:, s, :], w_raw[:, s, :], ACT.Copy).then_inc(w_hi_done, 1)

            def split(t, s, raws):
                act.wait_ge(tile_done, t - RING + 1)
                high_part(t, s, raws)

            for s in range(4):
                if s < LEAD:
                    high_part(s, s, 1)
                act.wait_ge(x_loaded[s], 16)
                nc.scalar.activation(x_hi[:, 2 * s:2 * s + 2, :], x_raw(s), ACT.Copy).then_inc(x_hi_done, 1)

            act.wait_ge(small_loaded, 48)
            with act.Fori(0, L1_TILES // RING) as g:
                for s in range(RING):
                    t = RING * g + s
                    high_part(t + LEAD, (s + LEAD) % RING, g + 1 + (s + LEAD) // RING)
                    act.wait_ge(tile_done, t + 1)
                    nc.scalar.activation(h_hi[:, ds(t, 1), :].rearrange("p a n -> p (a n)"), acc[s % 2][:, 0:N],
                                         ACT.Identity, bias=bcol[:, ds(t, 1)]).then_inc(acc_hi, 1)

            nc.scalar.activation(ew_abs[:, :], ew[:, :], ACT.Abs).then_inc(act_step, 1)
            act.wait_ge(act_step, 1)
            nc.scalar.activation(ew_exp[:, :], ew_abs[:, :], ACT.Exp, scale=-1.0).then_inc(act_step, 1)
            act.wait_ge(act_step, 2)
            nc.scalar.activation(ew_ln[:, :], ew_exp[:, :], ACT.Ln, bias=1.0).then_inc(soft_a, 1)

            for t in range(IV_TILE, PAIR_TILE):
                split(t + LEAD, (t + LEAD) % RING, (t + LEAD) // RING + 1)

            def evacuate(t, u, slot, which):
                act.wait_ge(tile_done, t + 1)
                nc.scalar.activation(qk_hi[:, 2 * slot + which, :], acc[which][:, 0:N], ACT.Identity,
                                     bias=bcol[:, ds(u, 1)]).then_inc(acc_hi, 1)

            def att_high(a):
                act.wait_ge(pv_done, 2 * NT * (a + 1))
                nc.scalar.activation(att_hi[:, ds(a, 1), :].rearrange("p a n -> p (a n)"), bank[5][:, 0:N],
                                     ACT.Copy).then_inc(att_hi_done, 1)

            def v_high(a, par):
                nc.scalar.activation(v_split(vp_hi, par), v_pair(a), ACT.Copy).then_inc(vp_hi_done, 1)

            def exps(a):
                for i in range(2 * NT):
                    act.wait_ge(masked, 2 * NT * a + (i + 1))
                    nc.scalar.activation(probs[:, i, :], probs[:, i, :], ACT.Exp, bias=neg_max[:, i:i + 1],
                                         scale=-1.0, accum_out=row_sum[:, i:i + 1]).then_inc(exp_done, 1)

            def pt_high(a):
                for g in range(2 * NT):
                    act.wait_ge(pt_ready, 2 * NT * a + (g + 1))
                    if g >= NT:
                        act.wait_ge(pv_done, 2 * NT * a + (g - NT + 1))
                    nc.scalar.activation(pt_hi[:, g % 3, :], bank[3 + g % 2][:, 0:N], ACT.Copy)\
                        .then_inc(pt_hi_done, 1)

            def step(j, par, first=0, more_tiles=True):
                t = PAIR_TILE + 2 * j
                a = j - 1
                s0 = (2 * par + LEAD) % RING
                raws = (t + LEAD) // RING + 1 if isinstance(j, int) else None
                if raws is None:
                    raws = first
                if not (isinstance(j, int) and j < 2):
                    att_high(a - 1)
                split(t + LEAD, s0, raws)
                if not (isinstance(j, int) and j < 1):
                    if isinstance(j, int) and a == 0:
                        act.wait_ge(v2_ready, 2 * NT)
                        act.dma_start(res[:, :, :], x_rows).then_inc(res_loaded, 16)
                        act.dma_start(row[:, :], bias_rows[1:2, :].to_broadcast([P, F])).then_inc(bo_loaded, 16)
                    v_high(a, 1 - par)
                    exps(a)
                if more_tiles:
                    evacuate(t, L1_TILES + 2 * j, par, 0)
                split(t + LEAD + 1, s0 + 1, raws)
                if not (isinstance(j, int) and j < 1):
                    pt_high(a)
                if more_tiles:
                    evacuate(t + 1, L1_TILES + 1 + 2 * j, par, 1)

            step(0, 0)
            step(1, 1)
            with act.Fori(1, PAIRS // 2) as jj:
                step(2 * jj, 0, first=jj + (PAIR_TILE + LEAD) // RING + 1)
                step(2 * jj + 1, 1, first=jj + (PAIR_TILE + 2 + LEAD) // RING + 1)
            step(PAIRS, 0, more_tiles=False)
            att_high(PAIRS - 1)
            for t in range(WO_TILE + RING, TILES):
                split(t, t % RING, t // RING + 1)
            for n in range(NT):
                act.wait_ge(var_ready, n + 1)
                nc.scalar.activation(std[:, n:n + 1], mean_var[:, n, 1:2], ACT.Sqrt, bias=LN_EPS)\
                    .then_inc(std_ready, 1)

        @block.vector
        def _(dve):
            steps = [0, 0]

            def then_settle(ins):
                steps[1] += 1
                ins.then_inc(dve_step, 1)
                dve.wait_ge(dve_step, steps[0] + steps[1])

            def new_part(before):
                steps[0], steps[1] = before, 0

            nc.vector.memset(vp_hi[:, :, :, D:2 * D].bitcast(F32), 0.0)
            nc.vector.memset(vp_lo[:, :, :, D:2 * D].bitcast(F32), 0.0).then_inc(acc_free, 2)
            nc.vector.memset(table[:, :, :], 0.0).then_inc(gathered, 1)
            nc.vector.memset(one_i[:, :], 1).then_inc(scattered, 1)
            nc.vector.memset(ident4[:, :], 0.0).then_inc(a_ready, 1)
            nc.vector.memset(table_bits[:, :, :], 0.0).then_inc(table_ready, 1)

            dve.wait_ge(edges_loaded, 32)
            then_settle(nc.vector.tensor_copy(er_src[:, :], er[:, 0, :]))
            nc.vector.scalar_tensor_tensor(out=er_key[:, :], in0=er[:, 0, :], scalar=float(N), in1=er[:, 1, :],
                                           op0=ALU.mult, op1=ALU.add).then_inc(edge_prep, 1)

            def low_part(t, s):
                dve.wait_ge(w_hi_done, t + 1)
                nc.vector.tensor_tensor(w_lo[:, s, POOL_COLS:F], w_raw[:, s, POOL_COLS:F],
                                        w_hi[:, s, POOL_COLS:F].bitcast(F32), ALU.subtract)\
                    .then_inc(w_lo_dve, 1)

            for s in range(4):
                if s < LEAD:
                    low_part(s, s)
                dve.wait_ge(x_hi_done, s + 1)
                nc.vector.tensor_tensor(x_lo[:, 2 * s:2 * s + 2, :], x_raw(s),
                                        x_hi[:, 2 * s:2 * s + 2, :].bitcast(F32), ALU.subtract)\
                    .then_inc(x_lo_done, 1)

            src_i, dst_i, typ_i = ec[:, 0, :], ec[:, 1, :], ec[:, 2, :]
            nc.vector.tensor_copy(srcf[:, :], src_i)
            nc.vector.scalar_tensor_tensor(out=key[:, :], in0=src_i, scalar=float(N), in1=dst_i,
                                           op0=ALU.mult, op1=ALU.add)
            nc.vector.tensor_scalar(dhi[:, :], dst_i, 3, None, ALU.logical_shift_right)
            nc.vector.tensor_scalar(four[:, :], typ_i, 0.0, float(ETYPES), ALU.is_equal, ALU.mult)
            then_settle(nc.vector.tensor_scalar(dlo[:, :], dst_i, PACK - 1, None, ALU.bitwise_and))
            nc.vector.tensor_tensor(bit[:, :], one_i[:, :], dlo[:, :], ALU.logical_shift_left)
            nc.vector.tensor_tensor(code_i[:, :], four[:, :], typ_i, ALU.add)
            then_settle(nc.vector.tensor_scalar(dlo3[:, :], dlo[:, :], 3.0, None, ALU.mult))
            then_settle(nc.vector.tensor_tensor(packed_i[:, :], code_i[:, :], dlo3[:, :], ALU.logical_shift_left))
            nc.vector.tensor_copy(bitf[:, :], bit[:, :])
            nc.vector.tensor_copy(codef[:, :], packed_i[:, :])
            dve.wait_ge(consts, 4)
            nc.vector.tensor_copy(iota_h[:, :], iota_i[:, :])
            then_settle(nc.vector.tensor_copy(node_f[:, :], node_i[:, :]))

            def one_hots_by_node(g, slot):
                dve.wait_ge(rows_loaded, 32 * g + 32)
                dve.wait_ge(gathered, g + 1)
                for t in range(NT):
                    ins = nc.vector.tensor_scalar(node_hot[:, t, :], srcb[:, slot, :].rearrange("p a e -> p (a e)"),
                                                  node_f[:, t:t + 1], None, ALU.is_equal)
                ins.then_inc(at_ready, 1)
                nc.vector.tensor_tensor(sel[:, :, :], iota_i[:, None, 0:DH].to_broadcast([P, GC, DH]),
                                        dhi[:, ds(GC * g, GC)].unsqueeze(2).to_broadcast([P, GC, DH]),
                                        ALU.is_equal)

            def count_later(g, slot, chunks):
                for c in chunks:
                    n = GE - P * c
                    dve.wait_ge(dve_step, steps[0] + steps[1] - 2)
                    steps[1] += 1
                    nc.vector.scalar_tensor_tensor(
                        out=unread[:, c % 3, 0:n], in0=keyb[:, slot, P * c:GE].rearrange("p a e -> p (a e)"),
                        scalar=key[:, ds(GC * g + c, 1)], in1=later[:, 0:n],
                        op0=ALU.is_equal, op1=ALU.mult, accum_out=n_later[:, c:c + 1]).then_inc(dve_step, 1)

            def one_hots_by_edge(g):
                dve.wait_ge(scattered, g + 1)
                for c in range(GC):
                    ins = nc.vector.tensor_scalar(edge_hot[:, c, :], iota_h[:, :], srcf[:, ds(GC * g + c, 1)], None,
                                                  ALU.is_equal)
                ins.then_inc(a_ready, 1)

            def choose(g):
                mine = ds(GC * g, GC)
                dve.wait_ge(gathered, g + 2)
                then_settle(nc.vector.tensor_tensor(picked[:, :, :], gather_ps, sel[:, :, :], ALU.mult))
                then_settle(nc.vector.reduce_sum(occ[:, :], picked[:, :, :], axis=AX_X))
                then_settle(nc.vector.tensor_copy(occ_i[:, :], occ[:, :]))
                then_settle(nc.vector.tensor_tensor(hit[:, :], occ_i[:, :], bit[:, mine], ALU.bitwise_and))
                then_settle(nc.vector.tensor_tensor(lose[:, :], hit[:, :], n_later[:, :], ALU.add))
                nc.vector.scalar_tensor_tensor(out=win_bit[:, :], in0=lose[:, :], scalar=0.0, in1=bitf[:, mine],
                                               op0=ALU.is_equal, op1=ALU.mult)
                then_settle(nc.vector.scalar_tensor_tensor(out=win_code[:, :], in0=lose[:, :], scalar=0.0,
                                                           in1=codef[:, mine], op0=ALU.is_equal, op1=ALU.mult))
                nc.vector.tensor_tensor(mov[:, :, BITS], sel[:, :, :],
                                        win_bit[:, :].unsqueeze(2).to_broadcast([P, GC, DH]), ALU.mult)
                nc.vector.tensor_tensor(mov[:, :, CODES], sel[:, :, :],
                                        win_code[:, :].unsqueeze(2).to_broadcast([P, GC, DH]), ALU.mult)\
                    .then_inc(mov_ready, 1)

            def add_to_table(g):
                dve.wait_ge(scattered, g + 2)
                then_settle(nc.vector.tensor_tensor(table[:, :, :], scatter_ps, table[:, :, :], ALU.add))
                nc.vector.tensor_copy(table_bits[:, :, :], table[:, :, BITS]).then_inc(table_ready, 1)

            def evacuate(t, s):
                dve.wait_ge(acc_hi, t + 1)
                nc.vector.scalar_tensor_tensor(
                    out=h_lo[:, ds(t, 1), :].rearrange("p a n -> p (a n)"), in0=acc[s % 2][:, 0:N],
                    scalar=bcol[:, ds(t, 1)],
                    in1=h_hi[:, ds(t, 1), :].rearrange("p a n -> p (a n)").bitcast(F32),
                    op0=ALU.add, op1=ALU.subtract).then_inc(acc_free, 1)

            dve.wait_ge(small_loaded, 48)
            before = steps[1]
            STEPS_PER_GROUP = 7 + GC
            with dve.Fori(0, GROUPS) as g:
                new_part(STEPS_PER_GROUP * g + before)
                t = RING * g
                slot = ds(g % 2, 1)
                low_part(t + LEAD, 2)
                one_hots_by_node(g, slot)
                count_later(g, slot, range(0, 3))
                evacuate(t, 0)
                low_part(t + LEAD + 1, 3)
                count_later(g, slot, range(3, GC))
                one_hots_by_edge(g)
                evacuate(t + 1, 1)
                low_part(t + LEAD + 2, 0)
                choose(g)
                evacuate(t + 2, 2)
                low_part(t + LEAD + 3, 1)
                add_to_table(g)
                evacuate(t + 3, 3)
                assert steps[1] == STEPS_PER_GROUP
            new_part(STEPS_PER_GROUP * GROUPS + before)

            def lows(t):
                low_part(t + LEAD, (t + LEAD) % RING)

            lows(IV_TILE)
            then_settle(nc.vector.tensor_copy(tab_i[:, :, :], table[:, :, CODES]))
            for r in range(PACK):
                ins = nc.vector.tensor_scalar(field[:, :, :, r], tab_i[:, :, :], 3 * r, PACK - 1,
                                              ALU.logical_shift_right, ALU.bitwise_and)
            then_settle(ins)
            lows(IV_TILE + 1)
            then_settle(nc.vector.tensor_copy(codes, field[:, :, :, :].rearrange("p t d r -> p t (d r)")))
            then_settle(nc.vector.tensor_scalar(ident4[:, :], ident[:, :], float(ETYPES), None, ALU.mult))
            for t in range(NT):
                ins = nc.vector.scalar_tensor_tensor(out=diag[:, t, :], in0=codes[:, t, t * P:(t + 1) * P],
                                                     scalar=0.0, in1=ident4[:, :], op0=ALU.is_equal,
                                                     op1=ALU.mult)
            then_settle(ins)
            for t in range(NT):
                block_t = codes[:, t, t * P:(t + 1) * P]
                ins = nc.vector.tensor_tensor(block_t, block_t, diag[:, t, :], ALU.add)
            then_settle(ins)
            lows(IV_TILE + 2)
            then_settle(nc.vector.tensor_scalar(ew_pos[:, :], ew[:, :], 0.0, None, ALU.max))
            dve.wait_ge(soft_a, 1)
            then_settle(nc.vector.tensor_tensor(soft[:, :], ew_ln[:, :], ew_pos[:, :], ALU.add))
            then_settle(nc.vector.tensor_scalar(soft[:, :], soft[:, :], 1.0 / SCALE, None, ALU.mult))
            then_settle(nc.vector.tensor_scalar(mask[:, :, :], codes, 0.0, NEG, ALU.is_equal, ALU.mult))
            for c in range(ETYPES):
                then_settle(nc.vector.tensor_scalar(pick1, codes, float(c + 1), soft[:, c:c + 1],
                                                    ALU.is_equal, ALU.mult))
                then_settle(nc.vector.tensor_tensor(mask[:, :, :], mask[:, :, :], pick1, ALU.add))
                lows(IV_TILE + 3 + c)
            lows(IV_TILE + 7)

            for n in range(NT):
                for h in range(2):
                    dve.wait_ge(v2_acc, 2 * n + h + 1)
                    nc.vector.tensor_tensor(v2[:, n, h * HALF:(h + 1) * HALF], bank[2 * n + h][:, :],
                                            row[:, h * HALF:(h + 1) * HALF], ALU.add).then_inc(v2_ready, 1)

            def evacuate_pair(u, slot, which):
                dve.wait_ge(acc_hi, u + 1)
                nc.vector.scalar_tensor_tensor(
                    out=qk_lo[:, 2 * slot + which, :], in0=acc[which][:, 0:N], scalar=bcol[:, ds(u, 1)],
                    in1=qk_hi[:, 2 * slot + which, :].bitcast(F32),
                    op0=ALU.add, op1=ALU.subtract).then_inc(acc_free, 1)

            def att_low(a):
                dve.wait_ge(att_hi_done, a + 1)
                nc.vector.tensor_tensor(att_lo[:, ds(a, 1), :].rearrange("p a n -> p (a n)"), bank[5][:, 0:N],
                                        att_hi[:, ds(a, 1), :].rearrange("p a n -> p (a n)").bitcast(F32),
                                        ALU.subtract).then_inc(att_lo_done, 1)

            def v_low(a, par):
                dve.wait_ge(vp_hi_done, a + 1)
                nc.vector.tensor_tensor(v_split(vp_lo, par), v_pair(a), v_split(vp_hi, par).bitcast(F32),
                                        ALU.subtract).then_inc(vp_lo_done, 1)

            def mask_scores(a, i):
                dve.wait_ge(scores_ready, 2 * NT * a + (i + 1))
                dve.sem_inc(scores_seen, 1)
                nc.vector.tensor_tensor_reduce(out=probs[:, i, :], in0=bank[i % 3][:, 0:N], in1=mask[:, i // 2, :],
                                               scale=-SCALE, scalar=3.0e38, op0=ALU.add, op1=ALU.min,
                                               accum_out=neg_max[:, i:i + 1]).then_inc(masked, 1)

            def normalise(a, b):
                dve.wait_ge(exp_done, 2 * NT * a + (2 * b + 2))
                then_settle(nc.vector.reciprocal(row_inv[:, 2 * b:2 * b + 2], row_sum[:, 2 * b:2 * b + 2]))
                for i in (2 * b, 2 * b + 1):
                    nc.vector.tensor_scalar(probs[:, i, :], probs[:, i, :], row_inv[:, i:i + 1], None,
                                            ALU.mult).then_inc(probs_ready, 1)

            def pt_low(a):
                for g in range(2 * NT):
                    dve.wait_ge(pt_hi_done, 2 * NT * a + (g + 1))
                    nc.vector.tensor_tensor(pt_lo[:, g % 3, :], bank[3 + g % 2][:, 0:N],
                                            pt_hi[:, g % 3, :].bitcast(F32), ALU.subtract)\
                        .then_inc(pt_lo_done, 1)

            def step(j, par, more_tiles=True):
                t = PAIR_TILE + 2 * j
                a = j - 1
                s0 = (2 * par + LEAD) % RING
                start = isinstance(j, int) and j < 1
                if not (isinstance(j, int) and j < 2):
                    att_low(a - 1)
                low_part(t + LEAD, s0)
                if not start:
                    v_low(a, 1 - par)
                    if not (isinstance(a, int) and a == 0):
                        dve.wait_ge(pt_ready, 2 * NT * a)
                    mask_scores(a, 0)
                    mask_scores(a, 1)
                    mask_scores(a, 2)
                    normalise(a, 0)
                    mask_scores(a, 3)
                    mask_scores(a, 4)
                    normalise(a, 1)
                    mask_scores(a, 5)
                    normalise(a, 2)
                if more_tiles:
                    evacuate_pair(L1_TILES + 2 * j, par, 0)
                low_part(t + LEAD + 1, s0 + 1)
                if not start:
                    pt_low(a)
                if more_tiles:
                    evacuate_pair(L1_TILES + 1 + 2 * j, par, 1)

            step(0, 0)
            step(1, 1)
            before = steps[0] + steps[1]
            with dve.Fori(1, PAIRS // 2) as jj:
                new_part(2 * NT * jj + (before - 2 * NT))
                step(2 * jj, 0)
                step(2 * jj + 1, 1)
                assert steps[1] == 2 * NT
            new_part(before + 2 * NT * (PAIRS // 2 - 1))
            step(PAIRS, 0, more_tiles=False)
            att_low(PAIRS - 1)
            for t in range(WO_TILE + RING, TILES):
                low_part(t, t % RING)

            dve.wait_ge(res_ready, NT)
            for n in range(NT):
                for h in range(2):
                    half = res[:, n, h * HALF:(h + 1) * HALF]
                    dve.wait_ge(y_ready, 2 * n + h + 1)
                    then_settle(nc.vector.tensor_tensor(half, y_bank(n, h)[:, :], half, ALU.add))
                    ins = nc.vector.bn_stats(stats[:, n, 6 * h:6 * h + 6], half)
                then_settle(ins)
                nc.vector.bn_aggr(mean_var[:, n, :], stats[:, n, :]).then_inc(var_ready, 1)
                dve.wait_ge(std_ready, n + 1)
                then_settle(nc.vector.reciprocal(rstd[:, n:n + 1], std[:, n:n + 1]))
                nc.vector.tensor_scalar(res[:, n, :], res[:, n, :], mean_var[:, n, 0:1], rstd[:, n:n + 1],
                                        ALU.subtract, ALU.mult).then_inc(out_ready, 1)

        @block.tensor
        def _(pe):
            def tile_ready(t):
                pe.wait_ge(w_lo_dve, t + 1)
                pe.wait_ge(w_lo_pool, t + 1)

            def by_outputs(out_ps, s, k, moving_hi, moving_lo):
                cols = slice(k * P, (k + 1) * P)
                pe.matmul(out_ps, w_hi[:, s, cols], moving_hi, start=(k == 0), stop=False)
                pe.matmul(out_ps, w_hi[:, s, cols], moving_lo, start=False, stop=False)
                return pe.matmul(out_ps, w_lo[:, s, cols], moving_hi, start=False, stop=(k == KT - 1))

            def by_nodes(banks, s, left_hi, left_lo, start, stop, signal):
                for i, (left, right) in enumerate(((left_hi, w_hi), (left_hi, w_lo), (left_lo, w_hi))):
                    for h in range(2):
                        ins = pe.matmul(banks[h][:, :], left, right[:, s, h * HALF:(h + 1) * HALF],
                                        start=(start and i == 0), stop=(stop and i == 2))
                        if stop and i == 2:
                            ins.then_inc(signal, 1)
                return ins

            def gather(g):
                pe.wait_ge(table_ready, g + 1)
                pe.wait_ge(at_ready, g + 1)
                for c in range(GC):
                    for t in range(NT):
                        ins = pe.matmul(gather_ps[:, c, :], node_hot[:, t, c * P:(c + 1) * P], table_bits[:, t, :],
                                        start=(t == 0), stop=(t == NT - 1))
                ins.then_inc(gathered, 1)

            def scatter(g):
                pe.wait_ge(a_ready, g + 2)
                pe.wait_ge(mov_ready, g + 1)
                for t in range(NT):
                    for c in range(GC):
                        ins = pe.matmul(scatter_ps[:, t, :], edge_hot[:, c, t * P:(t + 1) * P], mov[:, c, :],
                                        start=(c == 0), stop=(c == GC - 1))
                ins.then_inc(scattered, 1)

            pe.wait_ge(x_lo_done, 4)
            with pe.Fori(0, L1_TILES // RING) as g:
                for s in range(RING):
                    t = RING * g + s
                    tile_ready(t)
                    pe.wait_ge(acc_free, t + 1)
                    for k in range(KT):
                        ins = by_outputs(acc[s % 2][:, 0:N], s, k, x_hi[:, k, :], x_lo[:, k, :])
                    ins.then_inc(tile_done, 1)
                    if s == 0:
                        gather(g)
                    if s == 2:
                        scatter(g)

            pe.wait_ge(table_ready, GROUPS + 1)
            pe.wait_ge(acc_free, L1_TILES + 2)
            for k in range(KT):
                t = IV_TILE + k
                tile_ready(t)
                for n in range(NT):
                    cols = slice(n * P, (n + 1) * P)
                    ins = by_nodes(bank[2 * n:2 * n + 2], t % RING, h_hi[:, V0 + k, cols], h_lo[:, V0 + k, cols],
                                   k == 0, k == KT - 1, v2_acc)
                if k < KT - 1:
                    ins.then_inc(tile_done, 1)
                else:
                    pe.matmul(acc[0][:, 0:1], ident[:, :], ident[:, 0:1], start=True, stop=True)\
                      .then_inc(tile_done, 1)

            def scores(a, par, b):
                q = slice(b * P, (b + 1) * P)
                for h in range(2):
                    i = 2 * b + h
                    if not (isinstance(a, int) and a == 0 and i < 3):
                        pe.wait_ge(masked, 2 * NT * a + (i - 2))
                for n, (left, right) in enumerate(((qk_hi, qk_hi), (qk_hi, qk_lo), (qk_lo, qk_hi))):
                    for h in range(2):
                        i = 2 * b + h
                        rows = slice(h * D, (h + 1) * D)
                        ins = pe.matmul(bank[i % 3][:, 0:N], left[rows, 2 * par, q], right[rows, 2 * par + 1, :],
                                        start=(n == 0), stop=(n == 2))
                        if n == 2:
                            ins.then_inc(scores_ready, 1)

            def transposes(a, g):
                h, m = divmod(g, NT)
                pe.wait_ge(probs_ready, 2 * NT * a + (2 * NT - 1 + h))
                if not (isinstance(a, int) and a == 0 and g < 2):
                    pe.wait_ge(pt_lo_done, 2 * NT * a + (g - 1))
                for b in range(NT):
                    ins = pe.transpose(bank[3 + g % 2][:, b * P:(b + 1) * P],
                                       probs[:, 2 * b + h, m * P:(m + 1) * P], ident[:, :])
                ins.then_inc(pt_ready, 1)

            def values(a, par, g):
                h, m = divmod(g, NT)
                if g == 0:
                    pe.wait_ge(vp_lo_done, a + 1)
                    if not (isinstance(a, int) and a == 0):
                        pe.wait_ge(att_lo_done, a)
                pe.wait_ge(pt_lo_done, 2 * NT * a + (g + 1))
                cols = slice(h * D, h * D + 2 * D)
                for n, (left, right) in enumerate(((vp_hi, pt_hi), (vp_hi, pt_lo), (vp_lo, pt_hi))):
                    ins = pe.matmul(bank[5][:, 0:N], left[:, par, m, cols], right[:, g % 3, :],
                                    start=(g == 0 and n == 0), stop=(g == 2 * NT - 1 and n == 2))
                ins.then_inc(pv_done, 1)

            def step(j, par):
                start = isinstance(j, int) and j < 1
                a = j - 1
                t = PAIR_TILE + 2 * j
                for which in range(2):
                    tile_ready(t + which)
                    pe.wait_ge(acc_free, L1_TILES + 2 * j + (which + 1))
                    for k in range(KT):
                        ins = by_outputs(acc[which][:, 0:N], 2 * par + which, k, h_hi[:, which * KT + k, :],
                                         h_lo[:, which * KT + k, :])
                        if k == KT - 1:
                            ins.then_inc(tile_done, 1)
                        if start:
                            continue
                        if which == 0 and k in (1, 3, 5):
                            if k == 1:
                                pe.wait_ge(acc_free, L1_TILES + 2 + 2 * j)
                                if isinstance(a, int) and a == 0:
                                    pe.wait_ge(v2_ready, 2 * NT)
                            scores(a, 1 - par, k // 2)
                        if which == 1 and k >= 1:
                            if k < KT - 1:
                                transposes(a, k - 1)
                            if k >= 3:
                                values(a, 1 - par, k - 3)
                if not start:
                    values(a, 1 - par, 2 * NT - 1)

            step(0, 0)
            step(1, 1)
            with pe.Fori(1, PAIRS // 2) as jj:
                step(2 * jj, 0)
                step(2 * jj + 1, 1)

            a = PAIRS - 1
            pe.wait_ge(acc_free, L1_TILES + 2 + 2 * PAIRS)
            for b in range(NT):
                scores(a, 1, b)

            def project(n, k, start, stop):
                cols = slice(n * P, (n + 1) * P)
                return by_nodes([y_bank(n, 0), y_bank(n, 1)], k % RING, att_hi[:, k, cols], att_lo[:, k, cols],
                                start, stop, y_ready)

            pe.wait_ge(att_lo_done, PAIRS - 1)
            for k in range(RING):
                tile_ready(WO_TILE + k)
                project(0, k, k == 0, False)
            transposes(a, 0)
            transposes(a, 1)
            for g in range(2 * NT):
                values(a, 1, g)
                if g + 2 < 2 * NT:
                    transposes(a, g + 2)
            pe.wait_ge(masked, 2 * NT * PAIRS)
            pe.wait_ge(pt_lo_done, 2 * NT * PAIRS)
            for k in range(RING):
                project(1, k, k == 0, False)
                project(2, k, k == 0, False).then_inc(tile_done, 1)
            for n in range(NT):
                for k in range(RING, KT):
                    if n == 0:
                        tile_ready(WO_TILE + k)
                    if n == 0 and k == KT - 1:
                        pe.wait_ge(att_lo_done, PAIRS)
                    project(n, k, False, k == KT - 1)


_OUT = (N, F)


def kernel(x, src, dst, edge_type_5, L0_gnn_edge_type_weights, L0_gnn_wq, L0_gnn_bq, L0_gnn_wk, L0_gnn_bk,
           L0_gnn_wv, L0_gnn_bv, L0_gnn_wiq, L0_gnn_biq, L0_gnn_wik, L0_gnn_bik, L0_gnn_wiv, L0_gnn_biv,
           L0_gnn_wo, L0_gnn_bo):
    import concourse.bacc as _bacc
    from concourse.bass_utils import run_bass_kernel_spmd as _run

    def by_out(w):
        return np.asarray(w).reshape(KT, P, KT, P).transpose(0, 3, 2, 1).reshape(KT, P, F)

    def by_in(w):
        return np.asarray(w).T.reshape(KT, P, F)

    x = np.asarray(x)
    pairs = np.stack([by_out(L0_gnn_wiq), by_out(L0_gnn_wik)], axis=1).reshape(2 * PAIRS, P, F)
    weights = np.concatenate([by_out(L0_gnn_wq), by_out(L0_gnn_wk), by_out(L0_gnn_wv), by_in(L0_gnn_wiv), pairs,
                              by_in(L0_gnn_wo)])
    flat = [np.asarray(b).reshape(KT, P) for b in (L0_gnn_bq, L0_gnn_bk, L0_gnn_bv)]
    pair_b = np.stack([np.asarray(b).reshape(KT, P) for b in (L0_gnn_biq, L0_gnn_bik)], axis=1).reshape(-1, P)
    edges = np.stack([np.asarray(e) for e in (src, dst, edge_type_5)])
    edges = edges.reshape(3, GROUPS, GC, P)[:, ::-1].reshape(3, CHUNKS, P)
    arrays = {
        "x_t": x.T.reshape(KT, P, N).transpose(1, 0, 2),
        "x_rows": x.reshape(NT, P, F).transpose(1, 0, 2),
        "weights": weights,
        "bias_cols": np.concatenate([*flat, pair_b]).T,
        "bias_rows": np.stack([np.asarray(L0_gnn_biv), np.asarray(L0_gnn_bo)]),
        "edge_weights": np.asarray(L0_gnn_edge_type_weights).reshape(1, ETYPES),
        "edge_cols": edges.transpose(2, 0, 1),
        "edge_rows": edges[:2].transpose(1, 0, 2),
    }
    arrays = {n: np.ascontiguousarray(v) for n, v in arrays.items()}
    nc = _bacc.Bacc("TRN2", target_bir_lowering=False, num_devices=1)
    args = [nc.dram_tensor(n, v.shape, mybir.dt.from_np(v.dtype), kind="ExternalInput").ap()
            for n, v in arrays.items()]
    key_rows = nc.dram_tensor("key_rows", (GROUPS, GE), F32, kind="Internal").ap()
    src_rows = nc.dram_tensor("src_rows", (GROUPS, GE), FP16, kind="Internal").ap()
    out = nc.dram_tensor("out", _OUT, F32, kind="ExternalOutput").ap()
    gnn_layer(nc, *args, key_rows, src_rows, out)
    r = _run(nc, [arrays], core_ids=[0])
    return r.results[0]["out"]
```

```python
from contextlib import ExitStack

import concourse.bass as bass
import numpy as np
from concourse import mybir

F32 = mybir.dt.float32
F32R = mybir.dt.float32r
BF16 = mybir.dt.bfloat16
FP16 = mybir.dt.float16
I32 = mybir.dt.int32
ACT = mybir.ActivationFunctionType
ALU = mybir.AluOpType
AX_X = mybir.AxisListType.X
ds = bass.ds

P = 128
N = 384
NT = N // P
F = 1024
KT = F // P
HEADS = 16
D = F // HEADS
PAIRS = HEADS // 2
HALF = 512
ETYPES = 4
LN_EPS = 1e-5

E = 6144
CHUNKS = E // P
GC = 8
GROUPS = CHUNKS // GC
GE = GC * P
PACK = 8
DH = N // PACK

RING = 4
L1_TILES = 3 * KT
IV_TILE = L1_TILES
PAIR_TILE = IV_TILE + KT
WO_TILE = PAIR_TILE + 2 * PAIRS
TILES = WO_TILE + KT
LEAD = 2
POOL_COLS = 896
FIRST_COLS = 448
NEG = -3.0e38
SCALE = 1.0 / 8.0

BITS = slice(0, DH)
CODES = slice(DH, 2 * DH)


def gnn_layer(nc, x_t, x_rows, weights, bias_cols, bias_rows, edge_weights, edge_cols, edge_rows,
              key_rows, src_rows, out):
    with ExitStack() as ctx:
        def sb(name, shape, dt):
            return ctx.enter_context(nc.sbuf_tensor(name, shape, dt))

        def sem(name):
            return ctx.enter_context(nc.semaphore(name))

        x_hi, x_lo = sb("x_hi", [P, KT, N], F32R), sb("x_lo", [P, KT, N], F32R)
        att_hi, att_lo = x_hi, x_lo
        h_hi, h_lo = sb("h_hi", [P, L1_TILES, N], F32R), sb("h_lo", [P, L1_TILES, N], F32R)
        V0 = 2 * KT
        qk_hi, qk_lo = h_hi[:, V0:V0 + 4, :], h_lo[:, V0:V0 + 4, :]
        pt_hi, pt_lo = h_hi[:, V0 + 4:V0 + 7, :], h_lo[:, V0 + 4:V0 + 7, :]
        w_raw = sb("w_raw", [P, RING, F], F32)
        w_hi, w_lo = sb("w_hi", [P, RING, F], F32R), sb("w_lo", [P, RING, F], F32R)
        v2 = sb("v2", [P, NT, F], F32)
        vp_hi, vp_lo = sb("vp_hi", [P, 2, NT, 3 * D], F32R), sb("vp_lo", [P, 2, NT, 3 * D], F32R)
        probs = sb("probs", [P, 2 * NT, N], F32)
        mask = sb("mask", [P, NT, N], F32)
        ident = sb("ident", [P, P], F32)
        res = sb("res", [P, NT, F], F32)
        row = sb("row", [P, F], F32)
        bcol = sb("bcol", [P, L1_TILES + 2 * PAIRS], F32)
        neg_max, row_sum, row_inv = (sb(n, [P, 2 * NT], F32) for n in ("neg_max", "row_sum", "row_inv"))
        stats = sb("stats", [P, NT, 12], F32)
        mean_var = sb("mean_var", [P, NT, 2], F32)
        std = sb("std", [P, NT], F32)
        rstd = sb("rstd", [P, NT], F32)
        v2_flat = v2[:, :, :].rearrange("p a b -> p (a b)")

        def x_raw(s):
            return v2_flat[:, 2 * N * s:2 * N * (s + 1)].rearrange("p (k n) -> p k n", k=2)

        v2_16 = v2_flat.bitcast(BF16)
        node_hot = v2_16[:, 0:NT * GE].rearrange("p (t e) -> p t e", t=NT)
        edge_hot = v2_16[:, NT * GE:2 * NT * GE].rearrange("p (c s) -> p c s", c=GC)
        keyb = probs[:, :, :].rearrange("p a b -> p (a b)")[:, 0:2 * GE].rearrange("p (s e) -> p s e", s=2)
        res_flat = res[:, :, :].rearrange("p a b -> p (a b)")
        srcb = res_flat[:, 0:GE].bitcast(FP16).rearrange("p (s e) -> p s e", s=2)
        later = res_flat[:, GE:GE + GE // 2].bitcast(BF16)
        sel, picked = (res_flat[:, GE + GE // 2 + i * N:GE + GE // 2 + (i + 1) * N].rearrange("p (c d) -> p c d", c=GC)
                       for i in range(2))
        ec = sb("ec", [P, 3, CHUNKS], I32)
        er = sb("er", [CHUNKS, 2, P], I32)
        er_key = sb("er_key", [CHUNKS, P], F32)
        er_src = sb("er_src", [CHUNKS, P], FP16)
        src_neg, key = (sb(n, [P, CHUNKS], F32) for n in ("src_neg", "key"))
        dhi, dlo3, bit, one_i, code_i, packed_i = (
            sb(n, [P, CHUNKS], I32) for n in ("dhi", "dlo3", "bit", "one_i", "code_i", "packed_i"))
        dlo = sb("dlo", [P, CHUNKS], I32)
        four = sb("four", [P, CHUNKS], F32)
        bitf, codef = sb("bitf", [P, CHUNKS], F32), sb("codef", [P, CHUNKS], F32)
        iota_i = sb("iota_i", [P, N], I32)
        iota_h = sb("iota_h", [P, N], FP16)
        unread = res_flat[:, 3 * GE - 3 * GE // 4:3 * GE].bitcast(mybir.dt.uint8).rearrange("p (s e) -> p s e", s=3)
        node_i = sb("node_i", [P, NT], I32)
        node_f = sb("node_f", [P, NT], F32)
        mov = sb("mov", [P, GC, 2 * DH], BF16)
        table = sb("table", [P, NT, 2 * DH], F32)
        table_bits = sb("table_bits", [P, NT, DH], BF16)
        n_later = sb("n_later", [P, GC], F32)
        occ_i, hit = sb("occ_i", [P, GC], I32), sb("hit", [P, GC], I32)
        lose, win_bit, win_code = (sb(n, [P, GC], F32) for n in ("lose", "win_bit", "win_code"))
        ew, ew_abs, ew_exp, ew_ln, ew_pos, soft = (
            sb(n, [P, ETYPES], F32) for n in ("ew", "ew_abs", "ew_exp", "ew_ln", "ew_pos", "soft"))
        tab_i = sb("tab_i", [P, NT, DH], I32)
        ident4 = sb("ident4", [P, P], F32)
        diag = picked.rearrange("p c d -> p (c d)").rearrange("p (t n) -> p t n", t=NT)
        field = probs[:, 0:NT, :].bitcast(I32).rearrange("p t (d r) -> p t d r", r=PACK)
        pick1 = probs[:, 0:NT, :]
        codes = probs[:, NT:2 * NT, :]

        bank = [ctx.enter_context(nc.psum_tensor(f"bank{i}", [P, HALF], F32)) for i in range(8)]
        acc = bank[6:8]
        gather_ps = bank[5][:, 0:GC * DH].rearrange("p (c d) -> p c d", c=GC)
        scatter_ps, last_scatter_ps = (b[:, 0:NT * 2 * DH].rearrange("p (t d) -> p t d", t=NT)
                                       for b in (bank[4], acc[1]))

        def v_pair(a):
            return v2[:, :, ds(a * P, P)].rearrange("p n (h d) -> p n h d", h=2)

        def v_split(vp, par):
            return vp[:, par, :, :].rearrange("p n (z d) -> p n z d", z=3)[:, :, 0:3:2, :]

        def y_bank(n, h):
            return bank[6 + h] if n == 0 else bank[2 * (n - 1) + h]

        raw_loaded = [sem(f"raw_loaded{s}") for s in range(RING)]
        x_loaded = [sem(f"x_loaded{s}") for s in range(4)]
        small_loaded = sem("small_loaded")
        edges_loaded = sem("edges_loaded")
        scratch_stored = sem("scratch_stored")
        rows_loaded = sem("rows_loaded")
        res_loaded = sem("res_loaded")
        bo_loaded = sem("bo_loaded")
        x_hi_done, x_lo_done = sem("x_hi_done"), sem("x_lo_done")
        w_hi_done, w_lo_dve, w_lo_pool = sem("w_hi_done"), sem("w_lo_dve"), sem("w_lo_pool")
        tile_done = sem("tile_done")
        acc_hi = sem("acc_hi")
        acc_free = sem("acc_free")
        consts = sem("consts")
        consts_dve = sem("consts_dve")
        edge_prep = sem("edge_prep")
        at_ready, a_ready, mov_ready, table_ready = (
            sem(n) for n in ("at_ready", "a_ready", "mov_ready", "table_ready"))
        gathered, scattered = sem("gathered"), sem("scattered")
        soft_a, soft_b, soft_pos = sem("soft_a"), sem("soft_b"), sem("soft_pos")
        mask_built = sem("mask_built")
        v2_acc, v2_ready = sem("v2_acc"), sem("v2_ready")
        vp_hi_done, vp_lo_done = sem("vp_hi_done"), sem("vp_lo_done")
        scores_seen = sem("scores_seen")
        scores_ready, masked, exp_done, probs_ready = (
            sem(n) for n in ("scores_ready", "masked", "exp_done", "probs_ready"))
        pt_ready, pt_hi_done, pt_lo_done, pv_done = (
            sem(n) for n in ("pt_ready", "pt_hi_done", "pt_lo_done", "pv_done"))
        att_hi_done, att_lo_done = sem("att_hi_done"), sem("att_lo_done")
        res_ready = sem("res_ready")
        y_ready, var_ready, std_ready, out_ready = (
            sem(n) for n in ("y_ready", "var_ready", "std_ready", "out_ready"))
        stored = sem("stored")
        dve_step = sem("dve_step")
        act_step = sem("act_step")
        pool_step = sem("pool_step")

        block = ctx.enter_context(nc.Block())

        @block.sync
        def _(sp):
            for s in range(RING):
                sp.dma_start(w_raw[:, s, :], weights[s, :, :]).then_inc(raw_loaded[s], 16)
                if s == 0:
                    for p in range(4):
                        sp.dma_start(x_raw(p), x_t[:, 2 * p:2 * p + 2, :]).then_inc(x_loaded[p], 16)

            def load_tile(t, s):
                sp.wait_ge(w_hi_done, t - RING + 1)
                sp.wait_ge(w_lo_dve, t - RING + 1)
                sp.wait_ge(w_lo_pool, t - RING + 1)
                sp.dma_start(w_raw[:, s, :], weights[ds(t, 1), :, :].rearrange("a p n -> (a p) n"))\
                  .then_inc(raw_loaded[s], 16)

            def load_rows(g, slot):
                sp.dma_start(keyb[:, slot, :], key_rows[ds(g, 1), :].to_broadcast([P, GE]))\
                  .then_inc(rows_loaded, 16)
                sp.dma_start(srcb[:, slot, :], src_rows[ds(g, 1), :].to_broadcast([P, GE]))\
                  .then_inc(rows_loaded, 16)

            sp.wait_ge(edge_prep, 1)
            sp.dma_start(key_rows.rearrange("g (c e) -> (g c) e", e=P), er_key[:, :]).then_inc(scratch_stored, 16)
            sp.dma_start(src_rows.rearrange("g (c e) -> (g c) e", e=P), er_src[:, :]).then_inc(scratch_stored, 16)
            sp.wait_ge(scratch_stored, 32)
            load_rows(0, 0)
            with sp.Fori(1, GROUPS) as g:
                sp.wait_ge(rows_loaded, 32 * g)
                sp.wait_ge(mov_ready, g)
                load_rows(g, ds(g % 2, 1))
                for s in range(RING):
                    load_tile(4 * g + s, s)
            with sp.Fori(GROUPS, TILES // RING) as g:
                for s in range(RING):
                    load_tile(4 * g + s, s)
            for n in range(NT):
                for h in range(2):
                    half = slice(h * HALF, (h + 1) * HALF)
                    sp.wait_ge(out_ready, 2 * n + h + 1)
                    sp.dma_start(out[n * P:(n + 1) * P, half], res[:, n, half]).then_inc(stored, 16)
            sp.wait_ge(stored, 16 * 2 * NT)

        @block.gpsimd
        def _(pool):
            nc.gpsimd.iota(iota_i[:, :], pattern=[[1, N]], base=0, channel_multiplier=0).then_inc(consts, 1)
            nc.gpsimd.iota(node_i[:, :], pattern=[[P, NT]], base=0, channel_multiplier=1).then_inc(consts, 1)
            nc.gpsimd.memset(later[:, :], 1.0).then_inc(pool_step, 1)
            nc.gpsimd.memset(ident[:, :], 0.0).then_inc(pool_step, 1)
            pool.wait_ge(pool_step, 2)
            nc.gpsimd.affine_select(out=later[:, :], in_=later[:, :], compare_op=ALU.is_gt, fill=0.0, base=0,
                                    pattern=[[1, GE]], channel_multiplier=-1).then_inc(consts, 1)
            nc.gpsimd.affine_select(out=ident[:, :], in_=ident[:, :], compare_op=ALU.not_equal, fill=1.0, base=0,
                                    pattern=[[1, P]], channel_multiplier=-1).then_inc(consts, 1)

            for t in range(LEAD):
                pool.wait_ge(w_hi_done, t + 1)
                nc.gpsimd.tensor_tensor(w_lo[:, t, 0:FIRST_COLS], w_raw[:, t, 0:FIRST_COLS],
                                        w_hi[:, t, 0:FIRST_COLS].bitcast(F32), ALU.subtract).then_inc(w_lo_pool, 1)
            pool.wait_ge(x_lo_done, 4)
            nc.gpsimd.memset(edge_hot, 0.0).then_inc(a_ready, 1)

            def low_part(t, s):
                pool.wait_ge(w_hi_done, t + 1)
                nc.gpsimd.tensor_tensor(w_lo[:, s, 0:POOL_COLS], w_raw[:, s, 0:POOL_COLS],
                                        w_hi[:, s, 0:POOL_COLS].bitcast(F32), ALU.subtract)\
                    .then_inc(w_lo_pool, 1)

            def v_low(a, par):
                pool.wait_ge(vp_hi_done, a + 1)
                for n in range(NT):
                    ins = nc.gpsimd.tensor_tensor(v_split(vp_lo, par)[:, n, :, :], v_pair(a)[:, n, :, :],
                                                  v_split(vp_hi, par)[:, n, :, :].bitcast(F32), ALU.subtract)
                ins.then_inc(vp_lo_done, 1)

            with pool.Fori(0, (PAIR_TILE - IV_TILE + L1_TILES) // RING) as g:
                for s in range(RING):
                    low_part(RING * g + (s + LEAD), (s + LEAD) % RING)

            def step(j, par):
                t = PAIR_TILE + 2 * j
                s0 = (2 * par + LEAD) % RING
                if not (isinstance(j, int) and j == 0):
                    v_low(j - 1, 1 - par)
                low_part(t + LEAD, s0)
                low_part(t + LEAD + 1, s0 + 1)

            step(0, 0)
            step(1, 1)
            pool.wait_ge(res_loaded, 16)
            pool.wait_ge(bo_loaded, 16)
            for n in range(NT):
                nc.gpsimd.tensor_tensor(res[:, n, :], res[:, n, :], row[:, :], ALU.add).then_inc(res_ready, 1)
            with pool.Fori(1, PAIRS // 2) as jj:
                step(2 * jj, 0)
                step(2 * jj + 1, 1)
            step(PAIRS, 0)
            for t in range(WO_TILE + RING, TILES):
                low_part(t, t % RING)

        @block.scalar
        def _(act):
            act.dma_start(er[:, :, :], edge_rows).then_inc(edges_loaded, 16)
            act.dma_start(ec[:, :, :], edge_cols).then_inc(edges_loaded, 16)
            act.dma_start(ew[:, :], edge_weights.to_broadcast([P, ETYPES])).then_inc(small_loaded, 16)
            act.dma_start(bcol[:, :], bias_cols).then_inc(small_loaded, 16)
            act.dma_start(row[:, :], bias_rows[0:1, :].to_broadcast([P, F])).then_inc(small_loaded, 16)

            act.wait_ge(consts_dve, 1)
            nc.scalar.activation(std[:, 0:1], ident4[:, 0:1], ACT.Copy)

            def high_part(t, s, raws):
                act.wait_ge(raw_loaded[s], 16 * raws)
                nc.scalar.activation(w_hi[:, s, :], w_raw[:, s, :], ACT.Copy).then_inc(w_hi_done, 1)

            def split(t, s, raws):
                act.wait_ge(tile_done, t - RING + 1)
                high_part(t, s, raws)

            for s in range(4):
                if s < LEAD:
                    high_part(s, s, 1)
                act.wait_ge(x_loaded[s], 16)
                nc.scalar.activation(x_hi[:, 2 * s:2 * s + 2, :], x_raw(s), ACT.Copy).then_inc(x_hi_done, 1)

            act.wait_ge(small_loaded, 48)
            act.wait_ge(consts_dve, 2)
            with act.Fori(0, L1_TILES // RING) as g:
                for s in range(RING):
                    t = RING * g + s
                    high_part(t + LEAD, (s + LEAD) % RING, g + 1 + (s + LEAD) // RING)
                    act.wait_ge(tile_done, t + 1)
                    nc.scalar.activation(h_hi[:, ds(t, 1), :].rearrange("p a n -> p (a n)"), acc[s % 2][:, 0:N],
                                         ACT.Identity, bias=bcol[:, ds(t, 1)]).then_inc(acc_hi, 1)
                    if s == 1:
                        act.wait_ge(scattered, g + 1)
                    if s in (1, 2):
                        for c in range(GC // 2 * (s - 1), GC // 2 * s):
                            ins = nc.scalar.activation(edge_hot[:, c, :], iota_h[:, :], ACT.Square,
                                                       bias=src_neg[:, ds(GC * g + c, 1)])
                        ins.then_inc(act_step, 1)
                    if s == 3:
                        for c in range(2):
                            act.wait_ge(act_step, 2 * g + 2)
                            part = edge_hot[:, GC // 2 * c:GC // 2 * (c + 1), :]
                            ins = nc.scalar.activation(part, part, ACT.Relu, bias=1.0, scale=-1.0)
                        ins.then_inc(a_ready, 1)

            nc.scalar.activation(ew_abs[:, :], ew[:, :], ACT.Abs).then_inc(act_step, 1)
            act.wait_ge(act_step, 2 * GROUPS + 1)
            nc.scalar.activation(ew_exp[:, :], ew_abs[:, :], ACT.Exp, scale=-1.0).then_inc(act_step, 1)
            act.wait_ge(act_step, 2 * GROUPS + 2)
            nc.scalar.activation(ew_ln[:, :], ew_exp[:, :], ACT.Ln, bias=1.0).then_inc(soft_a, 1)

            for t in range(IV_TILE, PAIR_TILE):
                split(t + LEAD, (t + LEAD) % RING, (t + LEAD) // RING + 1)

            def evacuate(t, u, slot, which):
                act.wait_ge(tile_done, t + 1)
                nc.scalar.activation(qk_hi[:, 2 * slot + which, :], acc[which][:, 0:N], ACT.Identity,
                                     bias=bcol[:, ds(u, 1)]).then_inc(acc_hi, 1)

            def att_high(a):
                act.wait_ge(pv_done, 2 * NT * (a + 1))
                nc.scalar.activation(att_hi[:, ds(a, 1), :].rearrange("p a n -> p (a n)"), bank[5][:, 0:N],
                                     ACT.Copy).then_inc(att_hi_done, 1)

            def v_high(a, par):
                nc.scalar.activation(v_split(vp_hi, par), v_pair(a), ACT.Copy).then_inc(vp_hi_done, 1)

            def exps(a):
                for i in range(2 * NT):
                    act.wait_ge(masked, 2 * NT * a + (i + 1))
                    nc.scalar.activation(probs[:, i, :], probs[:, i, :], ACT.Exp, bias=neg_max[:, i:i + 1],
                                         scale=-1.0, accum_out=row_sum[:, i:i + 1]).then_inc(exp_done, 1)

            def pt_high(a, groups):
                for g in groups:
                    act.wait_ge(pt_ready, 2 * NT * a + (g + 1))
                    if g >= NT:
                        act.wait_ge(pv_done, 2 * NT * a + (g - NT + 1))
                    nc.scalar.activation(pt_hi[:, g % 3, :], bank[3 + g % 2][:, 0:N], ACT.Copy)\
                        .then_inc(pt_hi_done, 1)

            def step(j, par, first=0, more_tiles=True):
                t = PAIR_TILE + 2 * j
                a = j - 1
                s0 = (2 * par + LEAD) % RING
                raws = (t + LEAD) // RING + 1 if isinstance(j, int) else None
                if raws is None:
                    raws = first
                split(t + LEAD, s0, raws)
                if not (isinstance(j, int) and j < 1):
                    if isinstance(j, int) and a == 0:
                        act.wait_ge(v2_ready, 2 * NT)
                        act.dma_start(res[:, :, :], x_rows).then_inc(res_loaded, 16)
                        act.dma_start(row[:, :], bias_rows[1:2, :].to_broadcast([P, F])).then_inc(bo_loaded, 16)
                    v_high(a, 1 - par)
                    if not (isinstance(j, int) and j < 2):
                        att_high(a - 1)
                    exps(a)
                if more_tiles:
                    evacuate(t, L1_TILES + 2 * j, par, 0)
                split(t + LEAD + 1, s0 + 1, raws)
                attend = not (isinstance(j, int) and j < 1)
                if attend:
                    pt_high(a, range(2 * NT - 1))
                if more_tiles:
                    evacuate(t + 1, L1_TILES + 1 + 2 * j, par, 1)
                if attend:
                    pt_high(a, range(2 * NT - 1, 2 * NT))

            step(0, 0)
            step(1, 1)
            with act.Fori(1, PAIRS // 2) as jj:
                step(2 * jj, 0, first=jj + (PAIR_TILE + LEAD) // RING + 1)
                step(2 * jj + 1, 1, first=jj + (PAIR_TILE + 2 + LEAD) // RING + 1)
            step(PAIRS, 0, more_tiles=False)
            att_high(PAIRS - 1)
            for t in range(WO_TILE + RING, TILES):
                split(t, t % RING, t // RING + 1)
            for n in range(NT):
                act.wait_ge(var_ready, n + 1)
                nc.scalar.activation(std[:, n:n + 1], mean_var[:, n, 1:2], ACT.Sqrt, bias=LN_EPS)\
                    .then_inc(std_ready, 1)

        @block.vector
        def _(dve):
            steps = [0, 0]

            def then_settle(ins):
                steps[1] += 1
                ins.then_inc(dve_step, 1)
                dve.wait_ge(dve_step, steps[0] + steps[1])

            def new_part(before):
                steps[0], steps[1] = before, 0

            nc.vector.memset(ident4[:, :], 0.0).then_inc(consts_dve, 1)
            nc.vector.memset(vp_hi[:, :, :, D:2 * D].bitcast(F32), 0.0)
            nc.vector.memset(vp_lo[:, :, :, D:2 * D].bitcast(F32), 0.0).then_inc(acc_free, 2)
            nc.vector.memset(table[:, :, :], 0.0).then_inc(gathered, 1)
            nc.vector.memset(one_i[:, :], 1)
            nc.vector.memset(mov[:, :, :], 0.0).then_inc(mov_ready, 1)

            dve.wait_ge(edges_loaded, 32)
            then_settle(nc.vector.tensor_copy(er_src[:, :], er[:, 0, :]))
            nc.vector.scalar_tensor_tensor(out=er_key[:, :], in0=er[:, 0, :], scalar=float(N), in1=er[:, 1, :],
                                           op0=ALU.mult, op1=ALU.add).then_inc(edge_prep, 1)

            def low_part(t, s, cols=POOL_COLS):
                dve.wait_ge(w_hi_done, t + 1)
                nc.vector.tensor_tensor(w_lo[:, s, cols:F], w_raw[:, s, cols:F], w_hi[:, s, cols:F].bitcast(F32),
                                        ALU.subtract).then_inc(w_lo_dve, 1)

            for s in range(4):
                if s < LEAD:
                    low_part(s, s, FIRST_COLS)
                dve.wait_ge(x_hi_done, s + 1)
                nc.vector.tensor_tensor(x_lo[:, 2 * s:2 * s + 2, :], x_raw(s),
                                        x_hi[:, 2 * s:2 * s + 2, :].bitcast(F32), ALU.subtract)\
                    .then_inc(x_lo_done, 1)

            src_i, dst_i, typ_i = ec[:, 0, :], ec[:, 1, :], ec[:, 2, :]
            nc.vector.tensor_scalar(src_neg[:, :], src_i, -1.0, None, ALU.mult)
            nc.vector.scalar_tensor_tensor(out=key[:, :], in0=src_i, scalar=float(N), in1=dst_i,
                                           op0=ALU.mult, op1=ALU.add)
            nc.vector.tensor_scalar(dhi[:, :], dst_i, 3, None, ALU.logical_shift_right)
            nc.vector.tensor_scalar(four[:, :], typ_i, 0.0, float(ETYPES), ALU.is_equal, ALU.mult)
            then_settle(nc.vector.tensor_scalar(dlo[:, :], dst_i, PACK - 1, None, ALU.bitwise_and))
            nc.vector.tensor_tensor(bit[:, :], one_i[:, :], dlo[:, :], ALU.logical_shift_left)
            nc.vector.tensor_tensor(code_i[:, :], four[:, :], typ_i, ALU.add)
            then_settle(nc.vector.tensor_scalar(dlo3[:, :], dlo[:, :], 3.0, None, ALU.mult))
            then_settle(nc.vector.tensor_tensor(packed_i[:, :], code_i[:, :], dlo3[:, :], ALU.logical_shift_left))
            nc.vector.tensor_copy(bitf[:, :], bit[:, :])
            nc.vector.tensor_copy(codef[:, :], packed_i[:, :])
            dve.wait_ge(consts, 4)
            nc.vector.tensor_copy(iota_h[:, :], iota_i[:, :]).then_inc(consts_dve, 1)
            then_settle(nc.vector.tensor_copy(node_f[:, :], node_i[:, :]))

            def one_hots_by_node(g, slot):
                dve.wait_ge(rows_loaded, 32 * g + 32)
                dve.wait_ge(gathered, g + 1)
                for t in range(NT):
                    ins = nc.vector.tensor_scalar(node_hot[:, t, :], srcb[:, slot, :].rearrange("p a e -> p (a e)"),
                                                  node_f[:, t:t + 1], None, ALU.is_equal)
                ins.then_inc(at_ready, 1)
                dve.wait_ge(mov_ready, g + 1)
                nc.vector.tensor_tensor(sel[:, :, :], iota_i[:, None, 0:DH].to_broadcast([P, GC, DH]),
                                        dhi[:, ds(GC * g, GC)].unsqueeze(2).to_broadcast([P, GC, DH]),
                                        ALU.is_equal)

            def count_later(g, slot, chunks):
                for c in chunks:
                    n = GE - P * c
                    dve.wait_ge(dve_step, steps[0] + steps[1] - 2)
                    steps[1] += 1
                    nc.vector.scalar_tensor_tensor(
                        out=unread[:, c % 3, 0:n], in0=keyb[:, slot, P * c:GE].rearrange("p a e -> p (a e)"),
                        scalar=key[:, ds(GC * g + c, 1)], in1=later[:, 0:n],
                        op0=ALU.is_equal, op1=ALU.mult, accum_out=n_later[:, c:c + 1]).then_inc(dve_step, 1)

            def choose(g):
                mine = ds(GC * g, GC)
                dve.wait_ge(gathered, g + 2)
                then_settle(nc.vector.tensor_tensor(picked[:, :, :], gather_ps, sel[:, :, :], ALU.mult))
                with nc.allow_low_precision(reason="one term of each sum is not 0, and it is an integer below 256"):
                    then_settle(nc.vector.reduce_sum(occ_i[:, :], picked[:, :, :], axis=AX_X))
                then_settle(nc.vector.tensor_tensor(hit[:, :], occ_i[:, :], bit[:, mine], ALU.bitwise_and))
                then_settle(nc.vector.tensor_tensor(lose[:, :], hit[:, :], n_later[:, :], ALU.add))
                nc.vector.scalar_tensor_tensor(out=win_bit[:, :], in0=lose[:, :], scalar=0.0, in1=bitf[:, mine],
                                               op0=ALU.is_equal, op1=ALU.mult)
                then_settle(nc.vector.scalar_tensor_tensor(out=win_code[:, :], in0=lose[:, :], scalar=0.0,
                                                           in1=codef[:, mine], op0=ALU.is_equal, op1=ALU.mult))
                nc.vector.tensor_tensor(mov[:, :, BITS], sel[:, :, :],
                                        win_bit[:, :].unsqueeze(2).to_broadcast([P, GC, DH]), ALU.mult)
                nc.vector.tensor_tensor(mov[:, :, CODES], sel[:, :, :],
                                        win_code[:, :].unsqueeze(2).to_broadcast([P, GC, DH]), ALU.mult)\
                    .then_inc(mov_ready, 1)

            def add_to_table(g, sums):
                dve.wait_ge(scattered, g + 1)
                then_settle(nc.vector.tensor_tensor(table[:, :, :], sums, table[:, :, :], ALU.add))
                nc.vector.tensor_copy(table_bits[:, :, :], table[:, :, BITS]).then_inc(table_ready, 1)

            def evacuate(t, s):
                dve.wait_ge(acc_hi, t + 1)
                nc.vector.scalar_tensor_tensor(
                    out=h_lo[:, ds(t, 1), :].rearrange("p a n -> p (a n)"), in0=acc[s % 2][:, 0:N],
                    scalar=bcol[:, ds(t, 1)],
                    in1=h_hi[:, ds(t, 1), :].rearrange("p a n -> p (a n)").bitcast(F32),
                    op0=ALU.add, op1=ALU.subtract).then_inc(acc_free, 1)

            dve.wait_ge(small_loaded, 48)
            before = steps[1]
            STEPS_PER_GROUP = 6 + GC
            with dve.Fori(0, GROUPS) as g:
                new_part(STEPS_PER_GROUP * g + before)
                t = RING * g
                slot = ds(g % 2, 1)
                low_part(t + LEAD, 2)
                one_hots_by_node(g, slot)
                count_later(g, slot, range(0, 1))
                evacuate(t, 0)
                add_to_table(g, scatter_ps)
                low_part(t + LEAD + 1, 3)
                count_later(g, slot, range(1, 3))
                evacuate(t + 1, 1)
                low_part(t + LEAD + 2, 0)
                count_later(g, slot, range(3, GC))
                evacuate(t + 2, 2)
                choose(g)
                low_part(t + LEAD + 3, 1)
                evacuate(t + 3, 3)
                assert steps[1] == STEPS_PER_GROUP
            new_part(STEPS_PER_GROUP * GROUPS + before)

            def lows(t):
                low_part(t + LEAD, (t + LEAD) % RING)

            lows(IV_TILE)
            lows(IV_TILE + 1)
            add_to_table(GROUPS, last_scatter_ps)
            then_settle(nc.vector.tensor_copy(tab_i[:, :, :], table[:, :, CODES]))
            for r in range(PACK):
                ins = nc.vector.tensor_scalar(field[:, :, :, r], tab_i[:, :, :], 3 * r, PACK - 1,
                                              ALU.logical_shift_right, ALU.bitwise_and)
            then_settle(ins)
            then_settle(nc.vector.tensor_copy(codes, field[:, :, :, :].rearrange("p t d r -> p t (d r)")))
            then_settle(nc.vector.tensor_scalar(ident4[:, :], ident[:, :], float(ETYPES), None, ALU.mult))
            for t in range(NT):
                ins = nc.vector.scalar_tensor_tensor(out=diag[:, t, :], in0=codes[:, t, t * P:(t + 1) * P],
                                                     scalar=0.0, in1=ident4[:, :], op0=ALU.is_equal,
                                                     op1=ALU.mult)
            then_settle(ins)
            for t in range(NT):
                block_t = codes[:, t, t * P:(t + 1) * P]
                ins = nc.vector.tensor_tensor(block_t, block_t, diag[:, t, :], ALU.add)
            then_settle(ins)
            lows(IV_TILE + 2)
            then_settle(nc.vector.tensor_scalar(ew_pos[:, :], ew[:, :], 0.0, None, ALU.max))
            dve.wait_ge(soft_a, 1)
            then_settle(nc.vector.tensor_tensor(soft[:, :], ew_ln[:, :], ew_pos[:, :], ALU.add))
            then_settle(nc.vector.tensor_scalar(soft[:, :], soft[:, :], 1.0 / SCALE, None, ALU.mult))
            then_settle(nc.vector.tensor_scalar(mask[:, :, :], codes, 0.0, NEG, ALU.is_equal, ALU.mult))
            for c in range(ETYPES):
                then_settle(nc.vector.tensor_scalar(pick1, codes, float(c + 1), soft[:, c:c + 1],
                                                    ALU.is_equal, ALU.mult))
                then_settle(nc.vector.tensor_tensor(mask[:, :, :], mask[:, :, :], pick1, ALU.add))
                lows(IV_TILE + 3 + c)
            lows(IV_TILE + 7)

            for n in range(NT):
                for h in range(2):
                    if 2 * n + h < 5:
                        dve.wait_ge(v2_acc, 2 * n + h + 1)
                    else:
                        dve.wait_ge(tile_done, PAIR_TILE)
                    nc.vector.tensor_tensor(v2[:, n, h * HALF:(h + 1) * HALF], bank[2 * n + h][:, :],
                                            row[:, h * HALF:(h + 1) * HALF], ALU.add).then_inc(v2_ready, 1)

            def evacuate_pair(u, slot, which):
                dve.wait_ge(acc_hi, u + 1)
                nc.vector.scalar_tensor_tensor(
                    out=qk_lo[:, 2 * slot + which, :], in0=acc[which][:, 0:N], scalar=bcol[:, ds(u, 1)],
                    in1=qk_hi[:, 2 * slot + which, :].bitcast(F32),
                    op0=ALU.add, op1=ALU.subtract).then_inc(acc_free, 1)

            def att_low(a):
                dve.wait_ge(att_hi_done, a + 1)
                nc.vector.tensor_tensor(att_lo[:, ds(a, 1), :].rearrange("p a n -> p (a n)"), bank[5][:, 0:N],
                                        att_hi[:, ds(a, 1), :].rearrange("p a n -> p (a n)").bitcast(F32),
                                        ALU.subtract).then_inc(att_lo_done, 1)

            def mask_scores(a, i):
                dve.wait_ge(scores_ready, 2 * NT * a + (i + 1))
                dve.sem_inc(scores_seen, 1)
                nc.vector.tensor_tensor_reduce(out=probs[:, i, :], in0=bank[i % 3][:, 0:N], in1=mask[:, i // 2, :],
                                               scale=-SCALE, scalar=3.0e38, op0=ALU.add, op1=ALU.min,
                                               accum_out=neg_max[:, i:i + 1]).then_inc(masked, 1)

            def normalise(a, b):
                dve.wait_ge(exp_done, 2 * NT * a + (2 * b + 2))
                then_settle(nc.vector.reciprocal(row_inv[:, 2 * b:2 * b + 2], row_sum[:, 2 * b:2 * b + 2]))
                for i in (2 * b, 2 * b + 1):
                    nc.vector.tensor_scalar(probs[:, i, :], probs[:, i, :], row_inv[:, i:i + 1], None,
                                            ALU.mult).then_inc(probs_ready, 1)

            def pt_low(a, groups):
                for g in groups:
                    dve.wait_ge(pt_hi_done, 2 * NT * a + (g + 1))
                    nc.vector.tensor_tensor(pt_lo[:, g % 3, :], bank[3 + g % 2][:, 0:N],
                                            pt_hi[:, g % 3, :].bitcast(F32), ALU.subtract)\
                        .then_inc(pt_lo_done, 1)

            def step(j, par, more_tiles=True):
                t = PAIR_TILE + 2 * j
                a = j - 1
                s0 = (2 * par + LEAD) % RING
                start = isinstance(j, int) and j < 1
                if not (isinstance(j, int) and j < 2):
                    att_low(a - 1)
                low_part(t + LEAD, s0)
                if not start:
                    if not (isinstance(a, int) and a == 0):
                        dve.wait_ge(pt_ready, 2 * NT * a)
                    mask_scores(a, 0)
                    mask_scores(a, 1)
                    mask_scores(a, 2)
                    normalise(a, 0)
                    mask_scores(a, 3)
                    mask_scores(a, 4)
                    normalise(a, 1)
                    mask_scores(a, 5)
                    normalise(a, 2)
                low_part(t + LEAD + 1, s0 + 1)
                if more_tiles:
                    evacuate_pair(L1_TILES + 2 * j, par, 0)
                if not start:
                    pt_low(a, range(2 * NT - 1))
                if more_tiles:
                    evacuate_pair(L1_TILES + 1 + 2 * j, par, 1)
                if not start:
                    pt_low(a, range(2 * NT - 1, 2 * NT))

            step(0, 0)
            step(1, 1)
            before = steps[0] + steps[1]
            with dve.Fori(1, PAIRS // 2) as jj:
                new_part(2 * NT * jj + (before - 2 * NT))
                step(2 * jj, 0)
                step(2 * jj + 1, 1)
                assert steps[1] == 2 * NT
            new_part(before + 2 * NT * (PAIRS // 2 - 1))
            step(PAIRS, 0, more_tiles=False)
            att_low(PAIRS - 1)
            for t in range(WO_TILE + RING, TILES):
                low_part(t, t % RING)

            dve.wait_ge(res_ready, NT)
            for n in range(NT):
                for h in range(2):
                    half = res[:, n, h * HALF:(h + 1) * HALF]
                    dve.wait_ge(y_ready, 2 * n + h + 1)
                    then_settle(nc.vector.tensor_tensor(half, y_bank(n, h)[:, :], half, ALU.add))
                    ins = nc.vector.bn_stats(stats[:, n, 6 * h:6 * h + 6], half)
                then_settle(ins)
                nc.vector.bn_aggr(mean_var[:, n, :], stats[:, n, :]).then_inc(var_ready, 1)
                dve.wait_ge(std_ready, n + 1)
                then_settle(nc.vector.reciprocal(rstd[:, n:n + 1], std[:, n:n + 1]))
                for h in range(2):
                    half = res[:, n, h * HALF:(h + 1) * HALF]
                    nc.vector.tensor_scalar(half, half, mean_var[:, n, 0:1], rstd[:, n:n + 1],
                                            ALU.subtract, ALU.mult).then_inc(out_ready, 1)

        @block.tensor
        def _(pe):
            def tile_ready(t):
                pe.wait_ge(w_lo_dve, t + 1)
                pe.wait_ge(w_lo_pool, t + 1)

            def by_outputs(out_ps, s, k, moving_hi, moving_lo):
                cols = slice(k * P, (k + 1) * P)
                pe.matmul(out_ps, w_hi[:, s, cols], moving_hi, start=(k == 0), stop=False)
                pe.matmul(out_ps, w_hi[:, s, cols], moving_lo, start=False, stop=False)
                return pe.matmul(out_ps, w_lo[:, s, cols], moving_hi, start=False, stop=(k == KT - 1))

            def by_nodes(banks, s, left_hi, left_lo, start, stop, halves=(0, 1)):
                last = []
                for i, (left, right) in enumerate(((left_hi, w_hi), (left_hi, w_lo), (left_lo, w_hi))):
                    for h in halves:
                        ins = pe.matmul(banks[h][:, :], left, right[:, s, h * HALF:(h + 1) * HALF],
                                        start=(start and i == 0), stop=(stop and i == 2))
                        if i == 2:
                            last.append(ins)
                return last

            def gather(g):
                pe.wait_ge(table_ready, g + 1)
                pe.wait_ge(at_ready, g + 1)
                for c in range(GC):
                    for t in range(NT):
                        ins = pe.matmul(gather_ps[:, c, :], node_hot[:, t, c * P:(c + 1) * P], table_bits[:, t, :],
                                        start=(t == 0), stop=(t == NT - 1))
                ins.then_inc(gathered, 1)

            def scatter(g, sums):
                pe.wait_ge(a_ready, g + 1)
                pe.wait_ge(mov_ready, g + 1)
                for t in range(NT):
                    for c in range(GC):
                        ins = pe.matmul(sums[:, t, :], edge_hot[:, c, t * P:(t + 1) * P], mov[:, c, :],
                                        start=(c == 0), stop=(c == GC - 1))
                ins.then_inc(scattered, 1)

            with pe.Fori(0, L1_TILES // RING) as g:
                for s in range(RING):
                    t = RING * g + s
                    tile_ready(t)
                    pe.wait_ge(acc_free, t + 1)
                    for k in range(KT):
                        if s == 0 and k % 2 == 0:
                            pe.wait_ge(x_lo_done, k // 2 + 1)
                        ins = by_outputs(acc[s % 2][:, 0:N], s, k, x_hi[:, k, :], x_lo[:, k, :])
                    ins.then_inc(tile_done, 1)
                    if s == 0:
                        scatter(g, scatter_ps)
                    if s == 1:
                        gather(g)

            for k in range(KT):
                t = IV_TILE + k
                tile_ready(t)
                if k == 0:
                    pe.wait_ge(acc_free, L1_TILES + 1)
                if k == KT - 1:
                    pe.wait_ge(acc_free, L1_TILES + 2)
                for n in range(NT):
                    if k == 0 and n == 2:
                        pe.wait_ge(mov_ready, GROUPS + 1)
                    cols = slice(n * P, (n + 1) * P)
                    last = by_nodes(bank[2 * n:2 * n + 2], t % RING, h_hi[:, V0 + k, cols], h_lo[:, V0 + k, cols],
                                    k == 0, k == KT - 1)
                    if k == KT - 1:
                        last[0].then_inc(v2_acc, 1)
                        if n < NT - 1:
                            last[1].then_inc(v2_acc, 1)
                last[1].then_inc(tile_done, 1)
                if k == 0:
                    pe.wait_ge(acc_free, L1_TILES + 2)
                    scatter(GROUPS, last_scatter_ps)
            pe.wait_ge(table_ready, GROUPS + 1)

            def scores(a, par, b):
                q = slice(b * P, (b + 1) * P)
                for h in range(2):
                    i = 2 * b + h
                    if not (isinstance(a, int) and a == 0 and i < 3):
                        pe.wait_ge(masked, 2 * NT * a + (i - 2))
                for n, (left, right) in enumerate(((qk_hi, qk_hi), (qk_hi, qk_lo), (qk_lo, qk_hi))):
                    for h in range(2):
                        i = 2 * b + h
                        rows = slice(h * D, (h + 1) * D)
                        ins = pe.matmul(bank[i % 3][:, 0:N], left[rows, 2 * par, q], right[rows, 2 * par + 1, :],
                                        start=(n == 0), stop=(n == 2))
                        if n == 2:
                            ins.then_inc(scores_ready, 1)

            def transposes(a, g):
                h, m = divmod(g, NT)
                pe.wait_ge(probs_ready, 2 * NT * a + (2 * NT - 1 + h))
                if not (isinstance(a, int) and a == 0 and g < 2):
                    pe.wait_ge(pt_lo_done, 2 * NT * a + (g - 1))
                for b in range(NT):
                    ins = pe.transpose(bank[3 + g % 2][:, b * P:(b + 1) * P],
                                       probs[:, 2 * b + h, m * P:(m + 1) * P], ident[:, :])
                ins.then_inc(pt_ready, 1)

            def values(a, par, g):
                h, m = divmod(g, NT)
                if g == 0:
                    pe.wait_ge(vp_lo_done, a + 1)
                    if not (isinstance(a, int) and a == 0):
                        pe.wait_ge(att_lo_done, a)
                pe.wait_ge(pt_lo_done, 2 * NT * a + (g + 1))
                cols = slice(h * D, h * D + 2 * D)
                for n, (left, right) in enumerate(((vp_hi, pt_hi), (vp_hi, pt_lo), (vp_lo, pt_hi))):
                    ins = pe.matmul(bank[5][:, 0:N], left[:, par, m, cols], right[:, g % 3, :],
                                    start=(g == 0 and n == 0), stop=(g == 2 * NT - 1 and n == 2))
                ins.then_inc(pv_done, 1)

            def step(j, par):
                start = isinstance(j, int) and j < 1
                more = not (isinstance(j, int) and j < 2)
                a = j - 1
                t = PAIR_TILE + 2 * j
                for which in range(2):
                    tile_ready(t + which)
                    pe.wait_ge(acc_free, L1_TILES + 2 * j + (which + 1))
                    for k in range(KT):
                        ins = by_outputs(acc[which][:, 0:N], 2 * par + which, k, h_hi[:, which * KT + k, :],
                                         h_lo[:, which * KT + k, :])
                        if k == KT - 1:
                            ins.then_inc(tile_done, 1)
                        if start:
                            continue
                        if which == 0:
                            if more and k == 0:
                                values(a - 1, par, 2 * NT - 2)
                            if more and k == 1:
                                values(a - 1, par, 2 * NT - 1)
                            if k == 1:
                                pe.wait_ge(acc_free, L1_TILES + 2 + 2 * j)
                                if isinstance(a, int) and a == 0:
                                    pe.wait_ge(v2_ready, 2 * NT)
                            if k in (1, 3, 5):
                                scores(a, 1 - par, k // 2)
                        else:
                            if k >= 4:
                                values(a, 1 - par, k - 4)
                            if k >= 2:
                                transposes(a, k - 2)

            step(0, 0)
            step(1, 1)
            with pe.Fori(1, PAIRS // 2) as jj:
                step(2 * jj, 0)
                step(2 * jj + 1, 1)

            a = PAIRS - 1
            values(a - 1, 0, 2 * NT - 2)
            values(a - 1, 0, 2 * NT - 1)
            pe.wait_ge(acc_free, L1_TILES + 2 + 2 * PAIRS)

            def project(n, k, halves=(0, 1)):
                cols = slice(n * P, (n + 1) * P)
                return by_nodes([y_bank(n, 0), y_bank(n, 1)], k % RING, att_hi[:, k, cols], att_lo[:, k, cols],
                                k == 0, k == KT - 1, halves)

            pe.wait_ge(att_lo_done, RING)
            for k in range(RING):
                if k < NT:
                    scores(a, 1, k)
                tile_ready(WO_TILE + k)
                project(0, k)
            transposes(a, 0)
            transposes(a, 1)
            pe.wait_ge(masked, 2 * NT * PAIRS)
            for g in range(RING):
                project(1, g)
                values(a, 1, g)
                transposes(a, g + 2)
            values(a, 1, 2 * NT - 2)
            project(2, 0)[1].then_inc(tile_done, 1)
            values(a, 1, 2 * NT - 1)
            for k in range(1, RING):
                project(2, k)[1].then_inc(tile_done, 1)
            for n in range(NT - 1):
                for k in range(RING, KT):
                    if n == 0:
                        tile_ready(WO_TILE + k)
                        pe.wait_ge(att_lo_done, k + 1)
                    last = project(n, k)
                last[0].then_inc(y_ready, 1)
                last[1].then_inc(y_ready, 1)
            for h in range(2):
                for k in range(RING, KT):
                    last = project(NT - 1, k, (h,))
                last[0].then_inc(y_ready, 1)


_OUT = (N, F)


def kernel(x, src, dst, edge_type_5, L0_gnn_edge_type_weights, L0_gnn_wq, L0_gnn_bq, L0_gnn_wk, L0_gnn_bk,
           L0_gnn_wv, L0_gnn_bv, L0_gnn_wiq, L0_gnn_biq, L0_gnn_wik, L0_gnn_bik, L0_gnn_wiv, L0_gnn_biv,
           L0_gnn_wo, L0_gnn_bo):
    import concourse.bacc as _bacc
    from concourse.bass_utils import run_bass_kernel_spmd as _run

    def by_out(w):
        return np.asarray(w).reshape(KT, P, KT, P).transpose(0, 3, 2, 1).reshape(KT, P, F)

    def by_in(w):
        return np.asarray(w).T.reshape(KT, P, F)

    x = np.asarray(x)
    pairs = np.stack([by_out(L0_gnn_wiq), by_out(L0_gnn_wik)], axis=1).reshape(2 * PAIRS, P, F)
    weights = np.concatenate([by_out(L0_gnn_wq), by_out(L0_gnn_wk), by_out(L0_gnn_wv), by_in(L0_gnn_wiv), pairs,
                              by_in(L0_gnn_wo)])
    flat = [np.asarray(b).reshape(KT, P) for b in (L0_gnn_bq, L0_gnn_bk, L0_gnn_bv)]
    pair_b = np.stack([np.asarray(b).reshape(KT, P) for b in (L0_gnn_biq, L0_gnn_bik)], axis=1).reshape(-1, P)
    edges = np.stack([np.asarray(e) for e in (src, dst, edge_type_5)])
    edges = edges.reshape(3, GROUPS, GC, P)[:, ::-1].reshape(3, CHUNKS, P)
    arrays = {
        "x_t": x.T.reshape(KT, P, N).transpose(1, 0, 2),
        "x_rows": x.reshape(NT, P, F).transpose(1, 0, 2),
        "weights": weights,
        "bias_cols": np.concatenate([*flat, pair_b]).T,
        "bias_rows": np.stack([np.asarray(L0_gnn_biv), np.asarray(L0_gnn_bo)]),
        "edge_weights": np.asarray(L0_gnn_edge_type_weights).reshape(1, ETYPES),
        "edge_cols": edges.transpose(2, 0, 1),
        "edge_rows": edges[:2].transpose(1, 0, 2),
    }
    arrays = {n: np.ascontiguousarray(v) for n, v in arrays.items()}
    nc = _bacc.Bacc("TRN2", target_bir_lowering=False, num_devices=1)
    args = [nc.dram_tensor(n, v.shape, mybir.dt.from_np(v.dtype), kind="ExternalInput").ap()
            for n, v in arrays.items()]
    key_rows = nc.dram_tensor("key_rows", (GROUPS, GE), F32, kind="Internal").ap()
    src_rows = nc.dram_tensor("src_rows", (GROUPS, GE), FP16, kind="Internal").ap()
    out = nc.dram_tensor("out", _OUT, F32, kind="ExternalOutput").ap()
    gnn_layer(nc, *args, key_rows, src_rows, out)
    r = _run(nc, [arrays], core_ids=[0])
    return r.results[0]["out"]
```

```python
from contextlib import ExitStack

import concourse.bass as bass
import numpy as np
from concourse import mybir

F32 = mybir.dt.float32
F32R = mybir.dt.float32r
BF16 = mybir.dt.bfloat16
FP16 = mybir.dt.float16
I32 = mybir.dt.int32
ACT = mybir.ActivationFunctionType
ALU = mybir.AluOpType
AX_X = mybir.AxisListType.X
ds = bass.ds

P = 128
N = 384
NT = N // P
F = 1024
KT = F // P
HEADS = 16
D = F // HEADS
PAIRS = HEADS // 2
HALF = 512
ETYPES = 4
LN_EPS = 1e-5

E = 6144
CHUNKS = E // P
GC = 8
GROUPS = CHUNKS // GC
GE = GC * P
PACK = 8
DH = N // PACK

RING = 4
L1_TILES = 3 * KT
IV_TILE = L1_TILES
PAIR_TILE = IV_TILE + KT
WO_TILE = PAIR_TILE + 2 * PAIRS
TILES = WO_TILE + KT
LAST_TILES = TILES - RING
SCORE_PLACES = (3, 4, 5)
TRANSPOSES_FROM, VALUES_FROM = 2, 5
LEAD = 2
POOL_COLS = 832
FIRST_TILES, FIRST_COLS = LEAD + RING, 448
WARM_UP = 16
HALVES = (slice(0, HALF), slice(HALF, F))
V2_PIECES = [[(2 * n + h, HALVES[h]) for h in range(2)] for n in range(NT)]
OUT_PIECES = [[(6, HALVES[0]), (7, HALVES[1])], [(0, HALVES[0]), (1, HALVES[1])],
              [(2, HALVES[0]), (3, slice(HALF, F - HALF // 2)), (4, slice(F - HALF // 2, F))]]
NEG = -3.0e38
SCALE = 1.0 / 8.0

BITS = slice(0, DH)
CODES = slice(DH, 2 * DH)


def pool_cols(t):
    if isinstance(t, int) and t == 1:
        return slice(HALF, HALF + HALF // 2)
    return slice(0, FIRST_COLS if isinstance(t, int) and t < FIRST_TILES else POOL_COLS)


def gnn_layer(nc, x_t, x_rows, weights, bias_cols, bias_rows, edge_weights, edge_cols, edge_rows,
              key_rows, src_rows, out):
    with ExitStack() as ctx:
        def sb(name, shape, dt):
            return ctx.enter_context(nc.sbuf_tensor(name, shape, dt))

        def sem(name):
            return ctx.enter_context(nc.semaphore(name))

        x_hi, x_lo = sb("x_hi", [P, KT, N], F32R), sb("x_lo", [P, KT, N], F32R)
        att_hi, att_lo = x_hi, x_lo
        h_hi, h_lo = sb("h_hi", [P, L1_TILES, N], F32R), sb("h_lo", [P, L1_TILES, N], F32R)
        V0 = 2 * KT
        q_high, k_parts = h_hi[:, V0:V0 + 4, :], h_lo[:, V0:V0 + 4, :]
        q_low = h_hi[:, V0 + 7, :], h_lo[:, V0 + 7, :]
        pt_hi, pt_lo = h_hi[:, V0 + 4:V0 + 7, :], h_lo[:, V0 + 4:V0 + 7, :]
        w_raw = sb("w_raw", [P, RING, F], F32)
        w_hi, w_lo = sb("w_hi", [P, RING, F], F32R), sb("w_lo", [P, RING, F], F32R)
        v2 = sb("v2", [P, NT, F], F32)
        vp = sb("vp", [P, 2, NT, 6 * D], F32R)
        EVEN_HIGH, EVEN_LOW, ODD_LOW, ODD_HIGH, ZERO, ODD_AGAIN = range(6)
        probs = sb("probs", [P, 2 * NT, N], F32)
        mask = sb("mask", [P, NT, N], F32)
        ident = sb("ident", [P, P], F32)
        res = sb("res", [P, NT, F], F32)
        row = sb("row", [P, F], F32)
        bcol = sb("bcol", [P, L1_TILES + 2 * PAIRS], F32)
        neg_max, row_sum, row_inv = (sb(n, [P, 2 * NT], F32) for n in ("neg_max", "row_sum", "row_inv"))
        stats = sb("stats", [P, NT, 18], F32)
        mean_var = sb("mean_var", [P, NT, 2], F32)
        std = sb("std", [P, NT], F32)
        rstd, shift = sb("rstd", [P, NT], F32), sb("shift", [P, NT], F32)
        v2_flat = v2[:, :, :].rearrange("p a b -> p (a b)")

        h_hi_flat, h_lo_flat = (h[:, :, :].rearrange("p b n -> p (b n)") for h in (h_hi, h_lo))

        def w_part(t, s, cols):
            if isinstance(t, int) and t >= LAST_TILES:
                place = slice((t - LAST_TILES) * F + cols.start, (t - LAST_TILES) * F + cols.stop)
                return h_hi_flat[:, place], h_lo_flat[:, place]
            return w_hi[:, s, cols], w_lo[:, s, cols]

        def x_raw(k):
            return v2_flat[:, N * k:N * (k + 1)]

        v2_16 = v2_flat.bitcast(BF16)
        node_hot = v2_16[:, 0:NT * GE].rearrange("p (t e) -> p t e", t=NT)
        edge_hot = v2_16[:, NT * GE:2 * NT * GE].rearrange("p (c s) -> p c s", c=GC)
        keyb = probs[:, :, :].rearrange("p a b -> p (a b)")[:, 0:2 * GE].rearrange("p (s e) -> p s e", s=2)
        res_flat = res[:, :, :].rearrange("p a b -> p (a b)")
        srcb = res_flat[:, 0:GE].bitcast(FP16).rearrange("p (s e) -> p s e", s=2)
        later = res_flat[:, GE:GE + GE // 2].bitcast(BF16)
        sel, picked = (res_flat[:, GE + GE // 2 + i * N:GE + GE // 2 + (i + 1) * N].rearrange("p (c d) -> p c d", c=GC)
                       for i in range(2))
        ec = sb("ec", [P, 3, CHUNKS], I32)
        er = sb("er", [CHUNKS, 2, P], I32)
        er_key = sb("er_key", [CHUNKS, P], F32)
        er_src = sb("er_src", [CHUNKS, P], FP16)
        src_neg, key = (sb(n, [P, CHUNKS], F32) for n in ("src_neg", "key"))
        dhi, dlo3, bit, one_i, code_i, packed_i = (
            sb(n, [P, CHUNKS], I32) for n in ("dhi", "dlo3", "bit", "one_i", "code_i", "packed_i"))
        dlo = sb("dlo", [P, CHUNKS], I32)
        four = sb("four", [P, CHUNKS], F32)
        bitf, codef = sb("bitf", [P, CHUNKS], F32), sb("codef", [P, CHUNKS], F32)
        iota_i = sb("iota_i", [P, N], I32)
        iota_h = sb("iota_h", [P, N], FP16)
        unread = res_flat[:, 3 * GE - 3 * GE // 4:3 * GE].bitcast(mybir.dt.uint8).rearrange("p (s e) -> p s e", s=3)
        node_i = sb("node_i", [P, NT], I32)
        node_f = sb("node_f", [P, NT], F32)
        mov = sb("mov", [P, GC, 2 * DH], BF16)
        table = sb("table", [P, NT, 2 * DH], F32)
        table_bits = sb("table_bits", [P, NT, DH], BF16)
        n_later = sb("n_later", [P, GC], F32)
        occ_i, hit = sb("occ_i", [P, GC], I32), sb("hit", [P, GC], I32)
        lose, win_bit, win_code = (sb(n, [P, GC], F32) for n in ("lose", "win_bit", "win_code"))
        ew, ew_abs, ew_exp, ew_ln, ew_pos, soft = (
            sb(n, [P, ETYPES], F32) for n in ("ew", "ew_abs", "ew_exp", "ew_ln", "ew_pos", "soft"))
        tab_i = sb("tab_i", [P, NT, DH], I32)
        ident4 = sb("ident4", [P, P], F32)
        diag = picked.rearrange("p c d -> p (c d)").rearrange("p (t n) -> p t n", t=NT)
        att_half = iota_i[:, :].bitcast(F32)
        att_sum = mov[:, :, :].rearrange("p c d -> p (c d)").bitcast(F32)
        field = probs[:, 0:NT, :].bitcast(I32).rearrange("p t (d r) -> p t d r", r=PACK)
        pick1 = probs[:, 0:NT, :]
        codes = probs[:, NT:2 * NT, :]

        bank = [ctx.enter_context(nc.psum_tensor(f"bank{i}", [P, HALF], F32)) for i in range(8)]
        acc = bank[6:8]
        score_bank = [bank[i] for i in (0, 1, 2, 3, 0, 1)]

        def pt_bank(a, g):
            if isinstance(a, int) and a == PAIRS - 1:
                return bank[(2, 3)[g % 2]]
            return bank[(0, 2, 3)[g % 3]]

        out_bank = [bank[i] for i in (4, 5)]
        gather_ps = bank[5][:, 0:GC * DH].rearrange("p (c d) -> p c d", c=GC)
        scatter_ps, last_scatter_ps = (b[:, 0:NT * 2 * DH].rearrange("p (t d) -> p t d", t=NT)
                                       for b in (bank[4], acc[1]))

        def v_pair(a):
            return v2[:, :, ds(a * P, P)].rearrange("p n (h d) -> p n h d", h=2)

        def v_slots(par, first, last):
            step = last - first
            return vp[:, par, :, :].rearrange("p n (z d) -> p n z d", z=6)[:, :, first:last + 1:step, :]

        raw_loaded = [sem(f"raw_loaded{s}") for s in range(RING)]
        x_loaded = [sem(f"x_loaded{s}") for s in range(KT)]
        small_loaded = sem("small_loaded")
        edges_loaded = sem("edges_loaded")
        scratch_stored = sem("scratch_stored")
        rows_loaded = sem("rows_loaded")
        res_loaded = sem("res_loaded")
        biv_loaded, bo_loaded = sem("biv_loaded"), sem("bo_loaded")
        x_hi_done, x_lo_done = sem("x_hi_done"), sem("x_lo_done")
        w_hi_done, w_lo_dve, w_lo_pool = sem("w_hi_done"), sem("w_lo_dve"), sem("w_lo_pool")
        q_doubled = sem("q_doubled")
        first_half_hi, first_half_lo = sem("first_half_hi"), sem("first_half_lo")
        tile_done = sem("tile_done")
        acc_hi = sem("acc_hi")
        acc_free = sem("acc_free")
        consts = sem("consts")
        consts_dve = sem("consts_dve")
        edge_prep = sem("edge_prep")
        node_hot_ready, edge_hot_ready, mov_ready, table_ready = (
            sem(n) for n in ("node_hot_ready", "edge_hot_ready", "mov_ready", "table_ready"))
        gathered, scattered = sem("gathered"), sem("scattered")
        softplus_ln = sem("softplus_ln")
        v2_acc, v2_ready = sem("v2_acc"), sem("v2_ready")
        vp_hi_done, vp_done = sem("vp_hi_done"), sem("vp_done")
        scores_seen = sem("scores_seen")
        scores_ready, masked, exp_done, probs_ready = (
            sem(n) for n in ("scores_ready", "masked", "exp_done", "probs_ready"))
        pt_ready, pt_hi_done, pt_lo_done, pv_done = (
            sem(n) for n in ("pt_ready", "pt_hi_done", "pt_lo_done", "pv_done"))
        half_done, sum_done = sem("half_done"), sem("sum_done")
        att_hi_done, att_lo_done = sem("att_hi_done"), sem("att_lo_done")
        res_ready = sem("res_ready")
        y_ready, var_ready, std_ready, rstd_ready, out_act, out_dve = (
            sem(n) for n in ("y_ready", "var_ready", "std_ready", "rstd_ready", "out_act", "out_dve"))
        stored = sem("stored")
        dve_step = sem("dve_step")
        act_step = sem("act_step")
        pool_step = sem("pool_step")

        block = ctx.enter_context(nc.Block())

        @block.sync
        def _(sp):
            def first_tile(s):
                sp.dma_start(w_raw[:, s, :], weights[s, :, :]).then_inc(raw_loaded[s], 16)

            def load_tile(t, s):
                sp.wait_ge(w_hi_done, t - RING + 1)
                sp.wait_ge(w_lo_dve, t - RING + 1)
                sp.wait_ge(w_lo_pool, t - RING + 1)
                sp.dma_start(w_raw[:, s, :], weights[ds(t, 1), :, :].rearrange("a p n -> (a p) n"))\
                  .then_inc(raw_loaded[s], 16)

            def load_rows(g, slot):
                sp.dma_start(keyb[:, slot, :], key_rows[ds(g, 1), :].to_broadcast([P, GE]))\
                  .then_inc(rows_loaded, 16)
                sp.dma_start(srcb[:, slot, :], src_rows[ds(g, 1), :].to_broadcast([P, GE]))\
                  .then_inc(rows_loaded, 16)

            first_tile(0)
            for k in range(KT):
                sp.dma_start(x_raw(k), x_t[:, k, :]).then_inc(x_loaded[k], 16)
            first_tile(1)
            sp.dma_start(bcol[:, :], bias_cols).then_inc(small_loaded, 16)
            sp.dma_start(ew[:, :], edge_weights.to_broadcast([P, ETYPES])).then_inc(small_loaded, 16)
            sp.wait_ge(edge_prep, 1)
            sp.dma_start(key_rows.rearrange("g (c e) -> (g c) e", e=P), er_key[:, :]).then_inc(scratch_stored, 16)
            sp.dma_start(src_rows.rearrange("g (c e) -> (g c) e", e=P), er_src[:, :]).then_inc(scratch_stored, 16)
            first_tile(2)
            sp.wait_ge(scratch_stored, 32)
            load_rows(0, 0)
            first_tile(3)
            with sp.Fori(1, GROUPS) as g:
                for s in range(RING):
                    load_tile(RING * g + s, s)
                    if s == 1:
                        sp.wait_ge(rows_loaded, 32 * g)
                        sp.wait_ge(mov_ready, g)
                        load_rows(g, ds(g % 2, 1))
            sp.dma_start(row[:, :], bias_rows[0:1, :].to_broadcast([P, F])).then_inc(biv_loaded, 16)
            with sp.Fori(GROUPS, TILES // RING) as g:
                for s in range(RING):
                    load_tile(RING * g + s, s)
            for n in range(NT):
                for h, half in enumerate(HALVES):
                    if n < NT - 1:
                        sp.wait_ge(out_act, 2 * n + h + 1)
                    else:
                        sp.wait_ge((out_dve, out_act)[h], (1, 2 * n + 1)[h])
                    sp.dma_start(out[n * P:(n + 1) * P, half], res[:, n, half]).then_inc(stored, 16)
            sp.wait_ge(stored, 16 * 2 * NT)

        @block.gpsimd
        def _(pool):
            nc.gpsimd.iota(iota_i[:, :], pattern=[[1, N]], base=0, channel_multiplier=0).then_inc(consts, 1)
            nc.gpsimd.iota(node_i[:, :], pattern=[[P, NT]], base=0, channel_multiplier=1).then_inc(consts, 1)
            nc.gpsimd.memset(later[:, :], 1.0).then_inc(pool_step, 1)
            nc.gpsimd.memset(ident[:, :], 0.0).then_inc(pool_step, 1)
            pool.wait_ge(pool_step, 2)
            nc.gpsimd.affine_select(out=later[:, :], in_=later[:, :], compare_op=ALU.is_gt, fill=0.0, base=0,
                                    pattern=[[1, GE]], channel_multiplier=-1).then_inc(consts, 1)
            nc.gpsimd.affine_select(out=ident[:, :], in_=ident[:, :], compare_op=ALU.not_equal, fill=1.0, base=0,
                                    pattern=[[1, P]], channel_multiplier=-1).then_inc(consts, 1)

            def low_part(t, s):
                pool.wait_ge(w_hi_done, t + 1)
                cols = pool_cols(t)
                hi, lo = w_part(t, s, cols)
                nc.gpsimd.tensor_tensor(lo, w_raw[:, s, cols], hi.bitcast(F32), ALU.subtract)\
                    .then_inc(w_lo_pool, 1)

            def v_low(a, par):
                pool.wait_ge(vp_hi_done, a + 1)
                highs, lows = v_slots(par, EVEN_HIGH, ODD_HIGH), v_slots(par, EVEN_LOW, ODD_LOW)
                for n in range(NT):
                    nc.gpsimd.tensor_tensor(lows[:, n, :, :], v_pair(a)[:, n, :, :],
                                            highs[:, n, :, :].bitcast(F32), ALU.subtract)
                nc.gpsimd.tensor_copy(v_slots(par, ODD_AGAIN - 1, ODD_AGAIN)[:, :, 1, :],
                                      highs[:, :, 1, :].bitcast(F32)).then_inc(vp_done, 1)

            def att_low(a):
                pool.wait_ge(att_hi_done, a + 1)
                nc.gpsimd.tensor_tensor(att_lo[:, ds(a, 1), :].rearrange("p a n -> p (a n)"), att_sum,
                                        att_hi[:, ds(a, 1), :].rearrange("p a n -> p (a n)").bitcast(F32),
                                        ALU.subtract).then_inc(att_lo_done, 1)

            for t in range(FIRST_TILES):
                low_part(t, t % RING)
            with pool.Fori(1, PAIR_TILE // RING) as g:
                for s in range(RING):
                    low_part(RING * g + (s + LEAD), (s + LEAD) % RING)

            def step(j, par):
                t = PAIR_TILE + 2 * j
                s0 = (2 * par + LEAD) % RING
                if not (isinstance(j, int) and j == 0):
                    v_low(j - 1, 1 - par)
                low_part(t + LEAD, s0)
                if not (isinstance(j, int) and j < 2):
                    att_low(j - 2)
                low_part(t + LEAD + 1, s0 + 1)

            step(0, 0)
            step(1, 1)
            pool.wait_ge(res_loaded, 16)
            pool.wait_ge(bo_loaded, 16)
            with pool.Fori(1, PAIRS // 2) as jj:
                step(2 * jj, 0)
                block_n = res[:, ds(jj - 1, 1), :].rearrange("p a f -> p (a f)")
                nc.gpsimd.tensor_tensor(block_n, block_n, row[:, :], ALU.add).then_inc(res_ready, 1)
                step(2 * jj + 1, 1)
            assert PAIRS // 2 - 1 == NT
            low_part(WO_TILE + 2, 2)
            v_low(PAIRS - 1, 1)
            low_part(WO_TILE + 3, 3)
            for i in range(RING):
                if i == 1:
                    att_low(PAIRS - 2)
                if i == RING - 1:
                    att_low(PAIRS - 1)
                low_part(LAST_TILES + i, i)

        @block.scalar
        def _(act):
            act.dma_start(er[:, :, :], edge_rows).then_inc(edges_loaded, 16)
            act.dma_start(ec[:, :, :], edge_cols).then_inc(edges_loaded, 16)

            act.wait_ge(consts_dve, 1)
            nc.scalar.activation(std[:, 0:1], ident4[:, 0:1], ACT.Copy)

            def high_part(t, s, raws):
                act.wait_ge(raw_loaded[s], 16 * raws)
                nc.scalar.activation(w_part(t, s, slice(0, F))[0], w_raw[:, s, :], ACT.Copy).then_inc(w_hi_done, 1)

            def split(t, s, raws):
                act.wait_ge(tile_done, t - RING + 1)
                high_part(t, s, raws)

            high_part(0, 0, 1)
            for k in range(KT):
                act.wait_ge(x_loaded[k], 16)
                nc.scalar.activation(x_hi[:, k, :], x_raw(k), ACT.Copy).then_inc(x_hi_done, 1)
            act.wait_ge(raw_loaded[1], 16)
            for half, done in zip(HALVES, (first_half_hi, w_hi_done)):
                nc.scalar.activation(w_hi[:, 1, half], w_raw[:, 1, half], ACT.Copy).then_inc(done, 1)

            act.wait_ge(small_loaded, 32)

            def group(g, first=False):
                for s in range(RING):
                    t = RING * g + s
                    late = first and s < LEAD
                    if not late:
                        high_part(t + LEAD, (s + LEAD) % RING, g + 1 + (s + LEAD) // RING)
                    act.wait_ge(tile_done, t + 1)
                    nc.scalar.activation(h_hi[:, ds(t, 1), :].rearrange("p a n -> p (a n)"), acc[s % 2][:, 0:N],
                                         ACT.Identity, bias=bcol[:, ds(t, 1)]).then_inc(acc_hi, 1)
                    if late:
                        high_part(t + LEAD, s + LEAD, 1)
                    if s == 1:
                        if first:
                            act.wait_ge(x_lo_done, KT)
                            act.wait_ge(consts_dve, 2)
                        else:
                            act.wait_ge(scattered, g)
                    if s in (1, 2):
                        for c in range(GC // 2 * (s - 1), GC // 2 * s):
                            ins = nc.scalar.activation(edge_hot[:, c, :], iota_h[:, :], ACT.Square,
                                                       bias=src_neg[:, ds(GC * g + c, 1)])
                        ins.then_inc(act_step, 1)
                    if s == 3:
                        for c in range(2):
                            act.wait_ge(act_step, 2 * g + 2)
                            part = edge_hot[:, GC // 2 * c:GC // 2 * (c + 1), :]
                            ins = nc.scalar.activation(part, part, ACT.Relu, bias=1.0, scale=-1.0)
                        ins.then_inc(edge_hot_ready, 1)

            group(0, first=True)
            with act.Fori(1, GROUPS) as g:
                group(g)

            nc.scalar.activation(ew_abs[:, :], ew[:, :], ACT.Abs).then_inc(act_step, 1)
            act.wait_ge(act_step, 2 * GROUPS + 1)
            nc.scalar.activation(ew_exp[:, :], ew_abs[:, :], ACT.Exp, scale=-1.0).then_inc(act_step, 1)
            act.wait_ge(act_step, 2 * GROUPS + 2)
            nc.scalar.activation(ew_ln[:, :], ew_exp[:, :], ACT.Ln, bias=1.0).then_inc(softplus_ln, 1)

            for t in range(IV_TILE, PAIR_TILE):
                split(t + LEAD, (t + LEAD) % RING, (t + LEAD) // RING + 1)

            def evacuate(t, u, slot, which):
                act.wait_ge(tile_done, t + 1)
                for h in range(2):
                    here = slice(h * D, (h + 1) * D)
                    ins = nc.scalar.activation((q_high, k_parts)[which][here, 2 * slot + h, :],
                                               acc[which][here, 0:N], ACT.Identity, bias=bcol[here, ds(u, 1)])
                ins.then_inc(acc_hi, 1)

            def double(par, h):
                here, there = slice(h * D, (h + 1) * D), slice((1 - h) * D, (2 - h) * D)
                nc.scalar.activation(q_high[there, 2 * par + h, :], q_high[here, 2 * par + h, :].bitcast(F32),
                                     ACT.Copy).then_inc(q_doubled, 1)

            def att_half_out(a, h):
                pe_groups = 2 * NT * a + (NT + NT * h)
                act.wait_ge(pv_done, pe_groups)
                here, there = slice(h * D, (h + 1) * D), slice((1 - h) * D, (2 - h) * D)
                nc.scalar.activation(att_half[here, :], out_bank[h][there, 0:N], ACT.Copy).then_inc(half_done, 1)

            def att_high(a):
                act.wait_ge(sum_done, 2 * a + 2)
                nc.scalar.activation(att_hi[:, ds(a, 1), :].rearrange("p a n -> p (a n)"), att_sum,
                                     ACT.Copy).then_inc(att_hi_done, 1)

            def v_high(a, par):
                nc.scalar.activation(v_slots(par, EVEN_HIGH, ODD_HIGH), v_pair(a), ACT.Copy).then_inc(vp_hi_done, 1)

            def exps(a, tiles=range(2 * NT)):
                for i in tiles:
                    act.wait_ge(masked, 2 * NT * a + (i + 1))
                    nc.scalar.activation(probs[:, i, :], probs[:, i, :], ACT.Exp, bias=neg_max[:, i:i + 1],
                                         scale=-1.0, accum_out=row_sum[:, i:i + 1]).then_inc(exp_done, 1)

            def pt_high(a, groups):
                for g in groups:
                    act.wait_ge(pt_ready, 2 * NT * a + (g + 1))
                    if g >= NT:
                        act.wait_ge(pv_done, 2 * NT * a + (g - NT + 1))
                    nc.scalar.activation(pt_hi[:, g % 3, :], pt_bank(a, g)[:, 0:N], ACT.Copy)\
                        .then_inc(pt_hi_done, 1)

            def step(j, par, first=0):
                t = PAIR_TILE + 2 * j
                a = j - 1
                s0 = (2 * par + LEAD) % RING
                raws = (t + LEAD) // RING + 1 if isinstance(j, int) else first
                attend = not (isinstance(j, int) and j < 1)
                split(t + LEAD, s0, raws)
                if attend:
                    if isinstance(j, int) and a == 0:
                        act.wait_ge(v2_ready, 2 * NT)
                        act.dma_start(res[:, :, :], x_rows).then_inc(res_loaded, 16)
                        act.dma_start(row[:, :], bias_rows[1:2, :].to_broadcast([P, F])).then_inc(bo_loaded, 16)
                    v_high(a, 1 - par)
                    if isinstance(j, int) and j < 2:
                        exps(a)
                    else:
                        att_half_out(a - 1, 1)
                        exps(a)
                if attend:
                    pt_high(a, (0, 1))
                evacuate(t, L1_TILES + 2 * j, par, 0)
                act.wait_ge(acc_hi, L1_TILES + 1 + 2 * j)
                for h in range(2):
                    if attend:
                        pt_high(a, (2 + h,))
                    double(par, h)
                if not (isinstance(j, int) and j < 2):
                    att_high(a - 1)
                if attend:
                    pt_high(a, (4, 5))
                evacuate(t + 1, L1_TILES + 1 + 2 * j, par, 1)
                if attend:
                    att_half_out(a, 0)
                split(t + LEAD + 1, s0 + 1, raws)

            step(0, 0)
            step(1, 1)
            with act.Fori(1, PAIRS // 2) as jj:
                step(2 * jj, 0, first=jj + (PAIR_TILE + LEAD) // RING + 1)
                step(2 * jj + 1, 1, first=jj + (PAIR_TILE + 2 + LEAD) // RING + 1)

            a = PAIRS - 1
            split(WO_TILE + 2, 2, (WO_TILE + 2) // RING + 1)
            v_high(a, 1)
            att_half_out(a - 1, 1)
            exps(a, range(0, 3))
            split(WO_TILE + 3, 3, (WO_TILE + 3) // RING + 1)
            exps(a, range(3, 6))
            act.wait_ge(tile_done, WO_TILE)
            for i in range(RING):
                if i == 1:
                    pt_high(a, (0, 1))
                    att_high(a - 1)
                if i == 2:
                    pt_high(a, (4, 5))
                    att_half_out(a, 0)
                if i == 3:
                    att_half_out(a, 1)
                    att_high(a)
                high_part(LAST_TILES + i, i, LAST_TILES // RING + 1)
                if i == 1:
                    pt_high(a, (2, 3))

            for n in range(NT):
                act.wait_ge(var_ready, n + 1)
                nc.scalar.activation(std[:, n:n + 1], mean_var[:, n, 1:2], ACT.Sqrt, bias=LN_EPS)\
                    .then_inc(std_ready, 1)
                act.wait_ge(rstd_ready, n + 1)
                for half in HALVES if n < NT - 1 else HALVES[1:]:
                    nc.scalar.activation(res[:, n, half], res[:, n, half], ACT.Identity, bias=shift[:, n:n + 1],
                                         scale=rstd[:, n:n + 1]).then_inc(out_act, 1)

        @block.vector
        def _(dve):
            steps = [0, 0]

            def then_settle(ins):
                steps[1] += 1
                ins.then_inc(dve_step, 1)
                dve.wait_ge(dve_step, steps[0] + steps[1])

            def new_part(before):
                steps[0], steps[1] = before, 0

            nc.vector.memset(ident4[:, :], 0.0).then_inc(consts_dve, 1)
            nc.vector.memset(vp[:, :, :, ZERO * D:(ZERO + 1) * D].bitcast(F32), 0.0).then_inc(acc_free, 2)
            nc.vector.memset(table[:, :, :], 0.0).then_inc(gathered, 1)
            nc.vector.memset(one_i[:, :], 1).then_inc(mov_ready, 1)

            dve.wait_ge(edges_loaded, 32)
            then_settle(nc.vector.tensor_copy(er_src[:, :], er[:, 0, :]))
            nc.vector.scalar_tensor_tensor(out=er_key[:, :], in0=er[:, 0, :], scalar=float(N), in1=er[:, 1, :],
                                           op0=ALU.mult, op1=ALU.add).then_inc(edge_prep, 1)

            def low_part(t, s):
                dve.wait_ge(w_hi_done, t + 1)
                cols = slice(pool_cols(t).stop, F)
                hi, lo = w_part(t, s, cols)
                nc.vector.tensor_tensor(lo, w_raw[:, s, cols], hi.bitcast(F32), ALU.subtract)\
                    .then_inc(w_lo_dve, 1)

            low_part(0, 0)
            for k in range(KT):
                dve.wait_ge(x_hi_done, k + 1)
                nc.vector.tensor_tensor(x_lo[:, k, :], x_raw(k), x_hi[:, k, :].bitcast(F32),
                                        ALU.subtract).then_inc(x_lo_done, 1)
            half = HALVES[0]
            dve.wait_ge(first_half_hi, 1)
            nc.vector.tensor_tensor(w_lo[:, 1, half], w_raw[:, 1, half], w_hi[:, 1, half].bitcast(F32),
                                    ALU.subtract).then_inc(first_half_lo, 1)
            low_part(1, 1)

            src_i, dst_i, typ_i = ec[:, 0, :], ec[:, 1, :], ec[:, 2, :]
            nc.vector.tensor_scalar(src_neg[:, :], src_i, -1.0, None, ALU.mult)
            nc.vector.scalar_tensor_tensor(out=key[:, :], in0=src_i, scalar=float(N), in1=dst_i,
                                           op0=ALU.mult, op1=ALU.add)
            nc.vector.tensor_scalar(dhi[:, :], dst_i, 3, None, ALU.logical_shift_right)
            nc.vector.tensor_scalar(four[:, :], typ_i, 0.0, float(ETYPES), ALU.is_equal, ALU.mult)
            then_settle(nc.vector.tensor_scalar(dlo[:, :], dst_i, PACK - 1, None, ALU.bitwise_and))
            nc.vector.tensor_tensor(bit[:, :], one_i[:, :], dlo[:, :], ALU.logical_shift_left)
            nc.vector.tensor_tensor(code_i[:, :], four[:, :], typ_i, ALU.add)
            then_settle(nc.vector.tensor_scalar(dlo3[:, :], dlo[:, :], 3.0, None, ALU.mult))
            then_settle(nc.vector.tensor_tensor(packed_i[:, :], code_i[:, :], dlo3[:, :], ALU.logical_shift_left))
            nc.vector.tensor_copy(bitf[:, :], bit[:, :])
            nc.vector.tensor_copy(codef[:, :], packed_i[:, :])
            dve.wait_ge(consts, 4)
            nc.vector.tensor_copy(iota_h[:, :], iota_i[:, :]).then_inc(consts_dve, 1)
            then_settle(nc.vector.tensor_copy(node_f[:, :], node_i[:, :]))

            def one_hots_by_node(g, slot, first=False):
                dve.wait_ge(rows_loaded, 32 * g + 32)
                if not first:
                    dve.wait_ge(gathered, g)
                    for t in range(NT):
                        ins = nc.vector.tensor_scalar(node_hot[:, t, :],
                                                      srcb[:, slot, :].rearrange("p a e -> p (a e)"),
                                                      node_f[:, t:t + 1], None, ALU.is_equal)
                    ins.then_inc(node_hot_ready, 1)
                    dve.wait_ge(mov_ready, g + 1)
                nc.vector.tensor_tensor(sel[:, :, :], iota_i[:, None, 0:DH].to_broadcast([P, GC, DH]),
                                        dhi[:, ds(GC * g, GC)].unsqueeze(2).to_broadcast([P, GC, DH]),
                                        ALU.is_equal)

            def count_later(g, slot, chunks):
                for c in chunks:
                    n = GE - P * c
                    dve.wait_ge(dve_step, steps[0] + steps[1] - 2)
                    steps[1] += 1
                    nc.vector.scalar_tensor_tensor(
                        out=unread[:, c % 3, 0:n], in0=keyb[:, slot, P * c:GE].rearrange("p a e -> p (a e)"),
                        scalar=key[:, ds(GC * g + c, 1)], in1=later[:, 0:n],
                        op0=ALU.is_equal, op1=ALU.mult, accum_out=n_later[:, c:c + 1]).then_inc(dve_step, 1)

            def choose(g, first=False):
                mine = ds(GC * g, GC)
                lost = n_later
                if first:
                    dve.wait_ge(dve_step, steps[0] + steps[1])
                else:
                    dve.wait_ge(gathered, g + 1)
                    then_settle(nc.vector.tensor_tensor(picked[:, :, :], gather_ps, sel[:, :, :], ALU.mult))
                    with nc.allow_low_precision(reason="one term of each sum counts, an integer below 256"):
                        then_settle(nc.vector.reduce_sum(occ_i[:, :], picked[:, :, :], axis=AX_X))
                    then_settle(nc.vector.tensor_tensor(hit[:, :], occ_i[:, :], bit[:, mine], ALU.bitwise_and))
                    lost = lose
                    then_settle(nc.vector.tensor_tensor(lost[:, :], hit[:, :], n_later[:, :], ALU.add))
                nc.vector.scalar_tensor_tensor(out=win_bit[:, :], in0=lost[:, :], scalar=0.0, in1=bitf[:, mine],
                                               op0=ALU.is_equal, op1=ALU.mult)
                then_settle(nc.vector.scalar_tensor_tensor(out=win_code[:, :], in0=lost[:, :], scalar=0.0,
                                                           in1=codef[:, mine], op0=ALU.is_equal, op1=ALU.mult))
                nc.vector.tensor_tensor(mov[:, :, BITS], sel[:, :, :],
                                        win_bit[:, :].unsqueeze(2).to_broadcast([P, GC, DH]), ALU.mult)
                nc.vector.tensor_tensor(mov[:, :, CODES], sel[:, :, :],
                                        win_code[:, :].unsqueeze(2).to_broadcast([P, GC, DH]), ALU.mult)\
                    .then_inc(mov_ready, 1)

            def add_to_table(g, sums, cols=slice(0, 2 * DH)):
                dve.wait_ge(scattered, g)
                then_settle(nc.vector.tensor_tensor(table[:, :, cols], sums[:, :, cols], table[:, :, cols],
                                                    ALU.add))
                nc.vector.tensor_copy(table_bits[:, :, :], table[:, :, BITS]).then_inc(table_ready, 1)

            def evacuate(t, s):
                dve.wait_ge(acc_hi, t + 1)
                nc.vector.scalar_tensor_tensor(
                    out=h_lo[:, ds(t, 1), :].rearrange("p a n -> p (a n)"), in0=acc[s % 2][:, 0:N],
                    scalar=bcol[:, ds(t, 1)],
                    in1=h_hi[:, ds(t, 1), :].rearrange("p a n -> p (a n)").bitcast(F32),
                    op0=ALU.add, op1=ALU.subtract).then_inc(acc_free, 1)

            dve.wait_ge(small_loaded, 32)
            def group(g, slot, first=False):
                t = RING * g
                if first:
                    evacuate(t, 0)
                    low_part(t + LEAD, 2)
                    one_hots_by_node(g, slot, first)
                    count_later(g, slot, range(0, 1))
                else:
                    one_hots_by_node(g, slot)
                    low_part(t + LEAD, 2)
                    count_later(g, slot, range(0, 1))
                    evacuate(t, 0)
                    add_to_table(g, scatter_ps)
                if first:
                    evacuate(t + 1, 1)
                low_part(t + LEAD + 1, 3)
                count_later(g, slot, range(1, 3))
                if not first:
                    evacuate(t + 1, 1)
                count_later(g, slot, range(3, 5))
                low_part(t + LEAD + 2, 0)
                if first:
                    evacuate(t + 2, 2)
                count_later(g, slot, range(5, GC))
                if not first:
                    evacuate(t + 2, 2)
                choose(g, first)
                low_part(t + LEAD + 3, 1)
                evacuate(t + 3, 3)

            group(0, ds(0, 1), first=True)
            before = steps[1]
            STEPS_PER_GROUP = 6 + GC
            with dve.Fori(1, GROUPS) as g:
                new_part(STEPS_PER_GROUP * g + (before - STEPS_PER_GROUP))
                group(g, ds(g % 2, 1))
                assert steps[1] == STEPS_PER_GROUP
            new_part(STEPS_PER_GROUP * (GROUPS - 1) + before)

            def lows(t):
                low_part(t + LEAD, (t + LEAD) % RING)

            lows(IV_TILE)
            lows(IV_TILE + 1)
            add_to_table(GROUPS, last_scatter_ps, CODES)
            then_settle(nc.vector.tensor_copy(tab_i[:, :, :], table[:, :, CODES]))
            for r in range(PACK):
                ins = nc.vector.tensor_scalar(field[:, :, :, r], tab_i[:, :, :], 3 * r, PACK - 1,
                                              ALU.logical_shift_right, ALU.bitwise_and)
            then_settle(ins)
            then_settle(nc.vector.tensor_copy(codes, field[:, :, :, :].rearrange("p t d r -> p t (d r)")))
            then_settle(nc.vector.tensor_scalar(ident4[:, :], ident[:, :], float(ETYPES), None, ALU.mult))
            for t in range(NT):
                ins = nc.vector.scalar_tensor_tensor(out=diag[:, t, :], in0=codes[:, t, t * P:(t + 1) * P],
                                                     scalar=0.0, in1=ident4[:, :], op0=ALU.is_equal,
                                                     op1=ALU.mult)
            then_settle(ins)
            for t in range(NT):
                block_t = codes[:, t, t * P:(t + 1) * P]
                ins = nc.vector.tensor_tensor(block_t, block_t, diag[:, t, :], ALU.add)
            then_settle(ins)
            lows(IV_TILE + 2)
            then_settle(nc.vector.tensor_scalar(ew_pos[:, :], ew[:, :], 0.0, None, ALU.max))
            dve.wait_ge(softplus_ln, 1)
            then_settle(nc.vector.tensor_tensor(soft[:, :], ew_ln[:, :], ew_pos[:, :], ALU.add))
            then_settle(nc.vector.tensor_scalar(soft[:, :], soft[:, :], 1.0 / SCALE, None, ALU.mult))
            then_settle(nc.vector.tensor_scalar(mask[:, :, :], codes, 0.0, NEG, ALU.is_equal, ALU.mult))
            for c in range(ETYPES):
                then_settle(nc.vector.tensor_scalar(pick1, codes, float(c + 1), soft[:, c:c + 1],
                                                    ALU.is_equal, ALU.mult))
                then_settle(nc.vector.tensor_tensor(mask[:, :, :], mask[:, :, :], pick1, ALU.add))
                lows(IV_TILE + 3 + c)
            lows(IV_TILE + 7)

            dve.wait_ge(biv_loaded, 16)
            for n in range(NT):
                for h in range(2):
                    if 2 * n + h < 5:
                        dve.wait_ge(v2_acc, 2 * n + h + 1)
                    else:
                        dve.wait_ge(tile_done, PAIR_TILE)
                    nc.vector.tensor_tensor(v2[:, n, h * HALF:(h + 1) * HALF], bank[2 * n + h][:, :],
                                            row[:, h * HALF:(h + 1) * HALF], ALU.add).then_inc(v2_ready, 1)

            def evacuate_pair(u, slot, which):
                dve.wait_ge(acc_hi, u + 1)
                for h in range(2):
                    here, there = slice(h * D, (h + 1) * D), slice((1 - h) * D, (2 - h) * D)
                    low = k_parts[there, 2 * slot + h, :] if which else q_low[slot][here, :]
                    ins = nc.vector.scalar_tensor_tensor(
                        out=low, in0=acc[which][here, 0:N], scalar=bcol[here, ds(u, 1)],
                        in1=(q_high, k_parts)[which][here, 2 * slot + h, :].bitcast(F32),
                        op0=ALU.add, op1=ALU.subtract)
                ins.then_inc(acc_free, 1)

            def add_halves(a, h):
                dve.wait_ge(half_done, 2 * a + (h + 1))
                if h == 0 and not (isinstance(a, int) and a == 0):
                    dve.wait_ge(att_lo_done, a)
                here = slice(h * D, (h + 1) * D)
                nc.vector.tensor_tensor(att_sum[here, :], out_bank[h][here, 0:N], att_half[here, :], ALU.add)\
                    .then_inc(sum_done, 1)

            def mask_scores(a, i):
                dve.wait_ge(scores_ready, 2 * NT * a + (i + 1))
                dve.sem_inc(scores_seen, 1)
                nc.vector.tensor_tensor_reduce(out=probs[:, i, :], in0=score_bank[i][:, 0:N], in1=mask[:, i // 2, :],
                                               scale=-SCALE, scalar=3.0e38, op0=ALU.add, op1=ALU.min,
                                               accum_out=neg_max[:, i:i + 1]).then_inc(masked, 1)

            def normalise(a, tiles):
                dve.wait_ge(exp_done, 2 * NT * a + (tiles[-1] + 1))
                cols = slice(tiles[0], tiles[-1] + 1, 2)
                then_settle(nc.vector.reciprocal(row_inv[:, cols], row_sum[:, cols]))
                for i in tiles:
                    nc.vector.tensor_scalar(probs[:, i, :], probs[:, i, :], row_inv[:, i:i + 1], None,
                                            ALU.mult).then_inc(probs_ready, 1)

            def pt_low(a, groups):
                for g in groups:
                    dve.wait_ge(pt_hi_done, 2 * NT * a + (g + 1))
                    nc.vector.tensor_tensor(pt_lo[:, g % 3, :], pt_bank(a, g)[:, 0:N],
                                            pt_hi[:, g % 3, :].bitcast(F32), ALU.subtract)\
                        .then_inc(pt_lo_done, 1)

            def attention(a, u=None, par=None):
                if not (isinstance(a, int) and a == 0):
                    dve.wait_ge(pt_ready, 2 * NT * a)
                for i in range(5):
                    mask_scores(a, i)
                normalise(a, (0, 2))
                normalise(a, (4,))
                mask_scores(a, 5)
                if u is None:
                    low_part(WO_TILE + 3, 3)
                normalise(a, (1, 3))
                pt_low(a, (0,))
                normalise(a, (5,))
                pt_low(a, (1,))
                if not (isinstance(a, int) and a == 0):
                    add_halves(a - 1, 1)
                if u is None:
                    low_part(LAST_TILES, 0)
                pt_low(a, (2,))
                if u is not None:
                    evacuate_pair(u, par, 0)
                pt_low(a, (3,))

            def step(j, par):
                t = PAIR_TILE + 2 * j
                a = j - 1
                s0 = (2 * par + LEAD) % RING
                attend = not (isinstance(j, int) and j < 1)
                low_part(t + LEAD, s0)
                if attend:
                    attention(a, L1_TILES + 2 * j, par)
                    pt_low(a, (4, 5))
                else:
                    evacuate_pair(L1_TILES + 2 * j, par, 0)
                evacuate_pair(L1_TILES + 1 + 2 * j, par, 1)
                if attend:
                    add_halves(a, 0)
                low_part(t + LEAD + 1, s0 + 1)

            SOFTMAX_STEPS = 4
            step(0, 0)
            step(1, 1)
            before = steps[0] + steps[1]
            with dve.Fori(1, PAIRS // 2) as jj:
                new_part(2 * SOFTMAX_STEPS * jj + (before - 2 * SOFTMAX_STEPS))
                step(2 * jj, 0)
                step(2 * jj + 1, 1)
                assert steps[1] == 2 * SOFTMAX_STEPS
            new_part(before + 2 * SOFTMAX_STEPS * (PAIRS // 2 - 1))

            a = PAIRS - 1
            low_part(WO_TILE + 2, 2)
            attention(a)
            for i in range(1, RING):
                if i == 2:
                    pt_low(a, (4,))
                    add_halves(a, 0)
                    pt_low(a, (5,))
                if i == 3:
                    add_halves(a, 1)
                low_part(LAST_TILES + i, i)

            dve.wait_ge(res_ready, NT)
            for n in range(NT):
                for i, (b, cols) in enumerate(OUT_PIECES[n]):
                    part = res[:, n, cols]
                    dve.wait_ge(y_ready, 2 * n + i + 1)
                    then_settle(nc.vector.tensor_tensor(part, bank[b][:, 0:cols.stop - cols.start], part, ALU.add))
                    ins = nc.vector.bn_stats(stats[:, n, 6 * i:6 * i + 6], part)
                then_settle(ins)
                nc.vector.bn_aggr(mean_var[:, n, :], stats[:, n, 0:6 * i + 6]).then_inc(var_ready, 1)
                dve.wait_ge(std_ready, n + 1)
                then_settle(nc.vector.reciprocal(rstd[:, n:n + 1], std[:, n:n + 1]))
                nc.vector.scalar_tensor_tensor(out=shift[:, n:n + 1], in0=mean_var[:, n, 0:1], scalar=-1.0,
                                               in1=rstd[:, n:n + 1], op0=ALU.mult, op1=ALU.mult)\
                    .then_inc(rstd_ready, 1)
            left = res[:, n, HALVES[0]]
            nc.vector.tensor_scalar(left, left, mean_var[:, n, 0:1], rstd[:, n:n + 1],
                                    ALU.subtract, ALU.mult).then_inc(out_dve, 1)

        @block.tensor
        def _(pe):
            def tile_ready(t):
                pe.wait_ge(w_lo_dve, t + 1)
                pe.wait_ge(w_lo_pool, t + 1)

            def by_outputs(out_ps, s, k, moving_hi, moving_lo):
                cols = slice(k * P, (k + 1) * P)
                pe.matmul(out_ps, w_hi[:, s, cols], moving_hi, start=(k == 0), stop=False)
                pe.matmul(out_ps, w_hi[:, s, cols], moving_lo, start=False, stop=False)
                return pe.matmul(out_ps, w_lo[:, s, cols], moving_hi, start=False, stop=(k == KT - 1))

            def by_nodes(pieces, t, left_hi, left_lo, start, stop):
                last = []
                for i, (left, which) in enumerate(((left_hi, 0), (left_hi, 1), (left_lo, 0))):
                    for b, cols in pieces:
                        ins = pe.matmul(bank[b][:, 0:cols.stop - cols.start], left,
                                        w_part(t, t % RING, cols)[which],
                                        start=(start and i == 0), stop=(stop and i == 2))
                        if i == 2:
                            last.append(ins)
                return last

            def gather(g):
                pe.wait_ge(table_ready, g)
                pe.wait_ge(node_hot_ready, g)
                for c in range(GC):
                    for t in range(NT):
                        ins = pe.matmul(gather_ps[:, c, :], node_hot[:, t, c * P:(c + 1) * P], table_bits[:, t, :],
                                        start=(t == 0), stop=(t == NT - 1))
                ins.then_inc(gathered, 1)

            def scatter(g, sums, cols=slice(0, 2 * DH)):
                pe.wait_ge(edge_hot_ready, g)
                pe.wait_ge(mov_ready, g + 1)
                for t in range(NT):
                    for c in range(GC):
                        ins = pe.matmul(sums[:, t, cols], edge_hot[:, c, t * P:(t + 1) * P], mov[:, c, cols],
                                        start=(c == 0), stop=(c == GC - 1))
                ins.then_inc(scattered, 1)

            pe.wait_ge(consts_dve, 1)
            for i in range(WARM_UP):
                pe.matmul(acc[0][:, 0:P], ident4[:, :], ident4[:, :], start=True, stop=True)

            def group(g, first=False):
                for s in range(RING):
                    t = RING * g + s
                    by_halves = first and s == 1
                    if by_halves:
                        pe.wait_ge(first_half_lo, 1)
                    else:
                        tile_ready(t)
                    pe.wait_ge(acc_free, t + 1)
                    for k in range(KT):
                        if first and s == 0:
                            pe.wait_ge(x_lo_done, k + 1)
                        if by_halves and k == KT // 2:
                            tile_ready(t)
                        ins = by_outputs(acc[s % 2][:, 0:N], s, k, x_hi[:, k, :], x_lo[:, k, :])
                    ins.then_inc(tile_done, 1)
                    if s == 0 and not first:
                        scatter(g, scatter_ps)
                    if s == 1 and not first:
                        gather(g)

            group(0, first=True)
            with pe.Fori(1, GROUPS) as g:
                group(g)

            for k in range(KT):
                t = IV_TILE + k
                tile_ready(t)
                if k == 0:
                    pe.wait_ge(acc_free, L1_TILES + 1)
                if k == KT - 1:
                    pe.wait_ge(acc_free, L1_TILES + 2)
                for n in range(NT):
                    if k == 0 and n == 2:
                        pe.wait_ge(mov_ready, GROUPS + 1)
                    cols = slice(n * P, (n + 1) * P)
                    last = by_nodes(V2_PIECES[n], t, h_hi[:, V0 + k, cols], h_lo[:, V0 + k, cols],
                                    k == 0, k == KT - 1)
                    if k == KT - 1:
                        last[0].then_inc(v2_acc, 1)
                        if n < NT - 1:
                            last[1].then_inc(v2_acc, 1)
                last[1].then_inc(tile_done, 1)
                if k == 0:
                    pe.wait_ge(acc_free, L1_TILES + 2)
                    scatter(GROUPS, last_scatter_ps, CODES)
            pe.wait_ge(table_ready, GROUPS)

            def scores(a, par, b):
                q = slice(b * P, (b + 1) * P)
                if b == 0:
                    pe.wait_ge(q_doubled, 2 * a + 2)
                if b == 2:
                    pe.wait_ge(masked, 2 * NT * a + 2)
                for h in range(2):
                    pe.matmul(score_bank[2 * b + h][:, 0:N], q_high[:, 2 * par + h, q], k_parts[:, 2 * par + h, :],
                              start=True, stop=False)
                for h in range(2):
                    here = slice(h * D, (h + 1) * D)
                    pe.matmul(score_bank[2 * b + h][:, 0:N], q_low[par][here, q], k_parts[here, 2 * par + h, :],
                              start=False, stop=True).then_inc(scores_ready, 1)

            def transposes(a, g):
                h, m = divmod(g, NT)
                pe.wait_ge(probs_ready, 2 * NT * a + NT * (h + 1))
                for b in range(NT):
                    ins = pe.transpose(pt_bank(a, g)[:, b * P:(b + 1) * P],
                                       probs[:, 2 * b + h, m * P:(m + 1) * P], ident[:, :])
                ins.then_inc(pt_ready, 1)

            def values(a, par, g):
                h, m = divmod(g, NT)
                if g == 0:
                    pe.wait_ge(vp_done, a + 1)
                if m == 0 and not (isinstance(a, int) and a == 0):
                    pe.wait_ge(sum_done, 2 * a + (h - 1))
                pe.wait_ge(pt_lo_done, 2 * NT * a + (g + 1))

                def product(slots, pt, start=False, stop=False):
                    rows = D * len(slots)
                    return pe.matmul(out_bank[h][0:rows, 0:N], vp[:, par, m, slots.start * D:slots.stop * D],
                                     pt[:, g % 3, :], start=start, stop=stop)

                both = range(ODD_LOW, ODD_HIGH + 1) if h else range(EVEN_HIGH, EVEN_LOW + 1)
                high = range(ZERO, ODD_AGAIN + 1) if h else range(EVEN_HIGH, EVEN_HIGH + 1)
                if m < NT - 1:
                    product(both, pt_hi, start=(m == 0))
                    ins = product(high, pt_lo)
                else:
                    product(high, pt_lo)
                    ins = product(both, pt_hi, stop=True)
                ins.then_inc(pv_done, 1)

            def step(j, par):
                start = isinstance(j, int) and j < 1
                more = not (isinstance(j, int) and j < 2)
                a = j - 1
                t = PAIR_TILE + 2 * j
                for which in range(2):
                    tile_ready(t + which)
                    pe.wait_ge(acc_free, L1_TILES + 2 * j + (which + 1))
                    for k in range(KT):
                        ins = by_outputs(acc[which][:, 0:N], 2 * par + which, k, h_hi[:, which * KT + k, :],
                                         h_lo[:, which * KT + k, :])
                        if k == KT - 1:
                            ins.then_inc(tile_done, 1)
                        if start:
                            continue
                        if which == 0:
                            if more and KT - VALUES_FROM + k < 2 * NT:
                                values(a - 1, par, KT - VALUES_FROM + k)
                            if k == SCORE_PLACES[0]:
                                pe.wait_ge(acc_free, L1_TILES + 2 + 2 * j)
                                if isinstance(a, int) and a == 0:
                                    pe.wait_ge(v2_ready, 2 * NT)
                            if k in SCORE_PLACES:
                                scores(a, 1 - par, SCORE_PLACES.index(k))
                        else:
                            if k >= VALUES_FROM:
                                values(a, 1 - par, k - VALUES_FROM)
                            if 0 <= k - TRANSPOSES_FROM < 2 * NT:
                                transposes(a, k - TRANSPOSES_FROM)

            step(0, 0)
            step(1, 1)
            with pe.Fori(1, PAIRS // 2) as jj:
                step(2 * jj, 0)
                step(2 * jj + 1, 1)

            def project(n, k, pieces=slice(None)):
                if n == 0:
                    tile_ready(WO_TILE + k)
                    pe.wait_ge(att_lo_done, k + 1)
                cols = slice(n * P, (n + 1) * P)
                return by_nodes(OUT_PIECES[n][pieces], WO_TILE + k, att_hi[:, k, cols], att_lo[:, k, cols],
                                k == 0, k == KT - 1)

            a = PAIRS - 1
            left, right = slice(0, 1), slice(1, 2)
            pe.wait_ge(acc_free, L1_TILES + 1 + 2 * PAIRS)
            project(0, 0, left)
            for g in range(KT - VALUES_FROM, 2 * NT - 1):
                values(a - 1, 0, g)
            pe.wait_ge(acc_free, L1_TILES + 2 + 2 * PAIRS)
            scores(a, 1, 0)
            project(0, 0, right)
            values(a - 1, 0, 2 * NT - 1)
            scores(a, 1, 1)
            project(0, 1)
            scores(a, 1, 2)
            project(0, 2)
            pe.wait_ge(masked, 2 * NT * PAIRS - 1)
            project(1, 0, left)
            project(1, 1, left)
            transposes(a, 0)
            pe.wait_ge(masked, 2 * NT * PAIRS)
            project(1, 0, right)
            project(1, 1, right)
            project(1, 2)
            transposes(a, 1)
            project(0, 3)
            for g in range(4):
                values(a, 1, g)
                transposes(a, g + 2)
                project(*((1, 3), (0, 4), (1, 4), (0, 5))[g])
            values(a, 1, 4)
            project(1, 5)
            values(a, 1, 5)
            pe.wait_ge(sum_done, 2 * a + 1)
            project(2, 0)
            project(2, 1)
            project(2, 2)
            for k in range(6, KT):
                last = project(0, k)
            for ins in last:
                ins.then_inc(y_ready, 1)
            for k in range(6, KT):
                last = project(1, k)
            for ins in last:
                ins.then_inc(y_ready, 1)
            for i in range(len(OUT_PIECES[2])):
                for k in range(3, KT):
                    last = project(2, k, slice(i, i + 1))
                last[0].then_inc(y_ready, 1)


_OUT = (N, F)


def kernel(x, src, dst, edge_type_5, L0_gnn_edge_type_weights, L0_gnn_wq, L0_gnn_bq, L0_gnn_wk, L0_gnn_bk,
           L0_gnn_wv, L0_gnn_bv, L0_gnn_wiq, L0_gnn_biq, L0_gnn_wik, L0_gnn_bik, L0_gnn_wiv, L0_gnn_biv,
           L0_gnn_wo, L0_gnn_bo):
    import concourse.bacc as _bacc
    from concourse.bass_utils import run_bass_kernel_spmd as _run

    def by_out(w):
        return np.asarray(w).reshape(KT, P, KT, P).transpose(0, 3, 2, 1).reshape(KT, P, F)

    def by_in(w):
        return np.asarray(w).T.reshape(KT, P, F)

    x = np.asarray(x)
    pairs = np.stack([by_out(L0_gnn_wiq), by_out(L0_gnn_wik)], axis=1).reshape(2 * PAIRS, P, F)
    weights = np.concatenate([by_out(L0_gnn_wq), by_out(L0_gnn_wk), by_out(L0_gnn_wv), by_in(L0_gnn_wiv), pairs,
                              by_in(L0_gnn_wo)])
    flat = [np.asarray(b).reshape(KT, P) for b in (L0_gnn_bq, L0_gnn_bk, L0_gnn_bv)]
    pair_b = np.stack([np.asarray(b).reshape(KT, P) for b in (L0_gnn_biq, L0_gnn_bik)], axis=1).reshape(-1, P)
    edges = np.stack([np.asarray(e) for e in (src, dst, edge_type_5)])
    edges = edges.reshape(3, GROUPS, GC, P)[:, ::-1].reshape(3, CHUNKS, P)
    arrays = {
        "x_t": x.T.reshape(KT, P, N).transpose(1, 0, 2),
        "x_rows": x.reshape(NT, P, F).transpose(1, 0, 2),
        "weights": weights,
        "bias_cols": np.concatenate([*flat, pair_b]).T,
        "bias_rows": np.stack([np.asarray(L0_gnn_biv), np.asarray(L0_gnn_bo)]),
        "edge_weights": np.asarray(L0_gnn_edge_type_weights).reshape(1, ETYPES),
        "edge_cols": edges.transpose(2, 0, 1),
        "edge_rows": edges[:2].transpose(1, 0, 2),
    }
    arrays = {n: np.ascontiguousarray(v) for n, v in arrays.items()}
    nc = _bacc.Bacc("TRN2", target_bir_lowering=False, num_devices=1)
    args = [nc.dram_tensor(n, v.shape, mybir.dt.from_np(v.dtype), kind="ExternalInput").ap()
            for n, v in arrays.items()]
    key_rows = nc.dram_tensor("key_rows", (GROUPS, GE), F32, kind="Internal").ap()
    src_rows = nc.dram_tensor("src_rows", (GROUPS, GE), FP16, kind="Internal").ap()
    out = nc.dram_tensor("out", _OUT, F32, kind="ExternalOutput").ap()
    gnn_layer(nc, *args, key_rows, src_rows, out)
    r = _run(nc, [arrays], core_ids=[0])
    return r.results[0]["out"]
```
